# Optimizing a Trainium2 kernel written in Bass

```python
import numpy as np
import jax
import jax.numpy as jnp

def _softmax(x, axis=-1):
    return jax.nn.softmax(x, axis=axis)

def _gelu(x):
    return jax.nn.gelu(x, approximate=True)

def _silu(x):
    return jax.nn.silu(x)

def _sigmoid(x):
    return jax.nn.sigmoid(x)

def _layernorm(x, axis=-1, eps=1e-05):
    m = jnp.mean(x, axis=axis, keepdims=True)
    v = jnp.var(x, axis=axis, keepdims=True)
    return (x - m) / jnp.sqrt(v + eps)

def _scatter_add(tgt, idx, src, axis=0):
    return tgt.at[idx].add(src)

def _segment_sum(src, seg, n):
    return jax.ops.segment_sum(src, seg, n)
kernel_name = 'mk_sandwich_d1_jaxref_r8_cb19c7'

def setup_inputs(seed: int=0):
    np.random.seed(seed)
    _w = jnp.asarray

    def _L0_attn_setup():
        import jax, jax.numpy as jnp
        import numpy as np
        B, N, D_IN = (2, 256, 256)
        D_OUT, N_HEADS = (256, 16)
        D_HEAD = D_OUT // N_HEADS
        D_C_KV, D_C_Q = (64, 256)
        SCALE = D_HEAD ** 0.5
        key = jax.random.key(seed)
        ks = jax.random.split(key, 8)
        s = 0.02
        return {'x': jax.random.normal(ks[0], (B, N, D_IN), dtype=jnp.float32), 'W_DQ': jax.random.normal(ks[1], (D_C_Q, D_IN), dtype=jnp.float32) * s, 'W_UQ': jax.random.normal(ks[2], (D_OUT, D_C_Q), dtype=jnp.float32) * s, 'W_DKV': jax.random.normal(ks[3], (D_C_KV, D_IN), dtype=jnp.float32) * s, 'W_UK': jax.random.normal(ks[4], (D_OUT, D_C_KV), dtype=jnp.float32) * s, 'W_UV': jax.random.normal(ks[5], (D_OUT, D_C_KV), dtype=jnp.float32) * s, 'W_O': jax.random.normal(ks[6], (D_IN, D_OUT), dtype=jnp.float32) * s, 'b_O': jax.random.normal(ks[7], (D_IN,), dtype=jnp.float32) * s}
    _L0_attn_in = _L0_attn_setup()

    def _L0_ffn_setup():
        import jax, jax.numpy as jnp
        import numpy as np
        HIDDEN = 256
        INTER = 1024
        SCALE = 64.0

        def fwht(x):
            orig_shape = x.shape
            n = orig_shape[-1]
            x = x.reshape(-1, n)
            h = 1
            while h < n:
                x = x.reshape(-1, n // (2 * h), 2, h)
                a, b = (x[:, :, 0, :], x[:, :, 1, :])
                x = jnp.stack([a + b, a - b], axis=2).reshape(-1, n)
                h *= 2
            return (x / jnp.sqrt(jnp.asarray(n, x.dtype))).reshape(orig_shape)
        key = jax.random.key(seed)
        ks = jax.random.split(key, 8)
        inp = jax.random.normal(ks[0], (4, 256, HIDDEN), dtype=jnp.float32)
        SU_ug = jnp.where(jax.random.bernoulli(ks[1], 0.5, (HIDDEN,)), 1.0, -1.0).astype(jnp.float32)
        SU_dp = jnp.where(jax.random.bernoulli(ks[2], 0.5, (INTER,)), 1.0, -1.0).astype(jnp.float32)
        Wscale_ug = jax.random.uniform(ks[3], (2 * INTER,), jnp.float32, 0.5, 1.5)
        Wscale_dp = jax.random.uniform(ks[4], (HIDDEN,), jnp.float32, 0.5, 1.5)
        W_up = jax.random.normal(ks[5], (INTER, HIDDEN), dtype=jnp.float32) * 0.02
        W_gate = jax.random.normal(ks[6], (INTER, HIDDEN), dtype=jnp.float32) * 0.02
        W_down = jax.random.normal(ks[7], (HIDDEN, INTER), dtype=jnp.float32) * 0.02
        return {'input': inp, 'SU_ug': SU_ug, 'SU_dp': SU_dp, 'Wscale_ug': Wscale_ug, 'Wscale_dp': Wscale_dp, 'W_up': W_up, 'W_gate': W_gate, 'W_down': W_down}
    _L0_ffn_in = _L0_ffn_setup()
    _d = {'L0_attn_x': _L0_attn_in['x'], 'L0_attn_W_DQ': _L0_attn_in['W_DQ'], 'L0_attn_W_UQ': _L0_attn_in['W_UQ'], 'L0_attn_W_DKV': _L0_attn_in['W_DKV'], 'L0_attn_W_UK': _L0_attn_in['W_UK'], 'L0_attn_W_UV': _L0_attn_in['W_UV'], 'L0_attn_W_O': _L0_attn_in['W_O'], 'L0_attn_b_O': _L0_attn_in['b_O'], 'L0_ffn_SU_ug': _L0_ffn_in['SU_ug'], 'L0_ffn_SU_dp': _L0_ffn_in['SU_dp'], 'L0_ffn_Wscale_ug': _L0_ffn_in['Wscale_ug'], 'L0_ffn_Wscale_dp': _L0_ffn_in['Wscale_dp'], 'L0_ffn_W_up': _L0_ffn_in['W_up'], 'L0_ffn_W_gate': _L0_ffn_in['W_gate'], 'L0_ffn_W_down': _L0_ffn_in['W_down']}
    _x0 = _d['L0_attn_x']
    _d['L0_attn_x'] = jax.random.normal(jax.random.fold_in(jax.random.key(seed), 1), (4, 1024, 256), dtype=_x0.dtype)
    del _x0
    return _d

def reference(L0_attn_x, L0_attn_W_DQ, L0_attn_W_UQ, L0_attn_W_DKV, L0_attn_W_UK, L0_attn_W_UV, L0_attn_W_O, L0_attn_b_O, L0_ffn_SU_ug, L0_ffn_SU_dp, L0_ffn_Wscale_ug, L0_ffn_Wscale_dp, L0_ffn_W_up, L0_ffn_W_gate, L0_ffn_W_down):

    def _L0_attn_ref(x, W_DQ, W_UQ, W_DKV, W_UK, W_UV, W_O, b_O):
        import jax, jax.numpy as jnp
        import numpy as np
        B, N, D_IN = (2, 256, 256)
        D_OUT, N_HEADS = (256, 16)
        D_HEAD = D_OUT // N_HEADS
        D_C_KV, D_C_Q = (64, 256)
        SCALE = D_HEAD ** 0.5
        Bc, Nc, _ = x.shape
        c_q = jnp.einsum('bnc,qc->bnq', x, W_DQ)
        q = jnp.einsum('bnq,dq->bnd', c_q, W_UQ)
        c_kv = jnp.einsum('bnc,kc->bnk', x, W_DKV)
        k = jnp.einsum('bnk,dk->bnd', c_kv, W_UK)
        v = jnp.einsum('bnk,dk->bnd', c_kv, W_UV)
        q = q.reshape(Bc, Nc, N_HEADS, D_HEAD).transpose(0, 2, 1, 3)
        k = k.reshape(Bc, Nc, N_HEADS, D_HEAD).transpose(0, 2, 1, 3)
        v = v.reshape(Bc, Nc, N_HEADS, D_HEAD).transpose(0, 2, 1, 3)
        scores = jnp.einsum('bhqd,bhkd->bhqk', q, k) / SCALE
        causal = jnp.tril(jnp.ones((Nc, Nc), dtype=bool))
        scores = jnp.where(causal, scores, -jnp.inf)
        attn = jax.nn.softmax(scores, axis=-1)
        ctx = jnp.einsum('bhqk,bhkd->bhqd', attn, v)
        ctx = ctx.transpose(0, 2, 1, 3).reshape(Bc, Nc, D_OUT)
        return jnp.einsum('bnd,cd->bnc', ctx, W_O) + b_O

    def _L0_ffn_ref(input, SU_ug, SU_dp, Wscale_ug, Wscale_dp, W_up, W_gate, W_down):
        import jax, jax.numpy as jnp
        import numpy as np
        HIDDEN = 256
        INTER = 1024
        SCALE = 64.0

        def fwht(x):
            orig_shape = x.shape
            n = orig_shape[-1]
            x = x.reshape(-1, n)
            h = 1
            while h < n:
                x = x.reshape(-1, n // (2 * h), 2, h)
                a, b = (x[:, :, 0, :], x[:, :, 1, :])
                x = jnp.stack([a + b, a - b], axis=2).reshape(-1, n)
                h *= 2
            return (x / jnp.sqrt(jnp.asarray(n, x.dtype))).reshape(orig_shape)
        n = SU_ug.shape[0]
        x = input.reshape(-1, n)
        x = fwht(x * SU_ug) / SCALE
        x_up = x @ W_up.T * (Wscale_ug[:INTER] * SCALE)
        x_gate = x @ W_gate.T * (Wscale_ug[INTER:] * SCALE)
        x = jax.nn.silu(x_gate) * x_up
        x = fwht(x * SU_dp) / SCALE
        x = x @ W_down.T * (Wscale_dp * SCALE)
        return x.reshape(input.shape)
    x = L0_attn_x
    x = x + _layernorm(_L0_attn_ref(_layernorm(x, axis=-1), L0_attn_W_DQ, L0_attn_W_UQ, L0_attn_W_DKV, L0_attn_W_UK, L0_attn_W_UV, L0_attn_W_O, L0_attn_b_O), axis=-1)
    x = x + _layernorm(_L0_ffn_ref(_layernorm(x, axis=-1), L0_ffn_SU_ug, L0_ffn_SU_dp, L0_ffn_Wscale_ug, L0_ffn_Wscale_dp, L0_ffn_W_up, L0_ffn_W_gate, L0_ffn_W_down), axis=-1)
    return x

_drawn_inputs = setup_inputs


def setup_inputs(seed=0):
    import zlib

    import numpy as np

    out = dict(_drawn_inputs(seed))
    spreads = {}
    factors = {'L0_attn_W_DQ': 8.0, 'L0_attn_W_UQ': 8.0, 'L0_attn_W_UK': 8.0}
    for name, (base, spread) in spreads.items():
        noise = np.random.default_rng([zlib.crc32(name.encode()), seed]).standard_normal(out[name].shape)
        drawn = base * np.exp(spread * noise) if base else spread * noise
        out[name] = jnp.asarray(drawn.astype(out[name].dtype))
    for name, factor in factors.items():
        out[name] = (out[name] * factor).astype(out[name].dtype)
    return out
```

```python
from contextlib import ExitStack

import concourse.bass as bass
from concourse import mybir

P = 128
B, N, D = 4, 1024, 256
H, DH = 16, 16
CKV = 64
J = 1024
TT = N // P
CH = 512
NCH = N // CH
TC = CH // P
DT = D // P
JT = J // P
QUAD = 4
QUADS = H // QUAD
VW = DH + 1
STRIPS = [(0, 0), (0, 1), (0, 2), (1, 0), (1, 1), (2, 0)]
KS = len(STRIPS) * DH
KM = KS + 3
EPS = 1e-5
MASKED = -3.0e38

F32 = mybir.dt.float32
BF16 = mybir.dt.bfloat16
ALU = mybir.AluOpType
ACT = mybir.ActivationFunctionType
AX_X = mybir.AxisListType.X



def score_pieces():
    return [(h, qt, k0, min((qt + 1) * P - k0, CH))
            for h in range(QUAD) for qt in range(TT) for k0 in range(0, (qt + 1) * P, CH)]


def maxima(ahead, quad):
    return [("sa", ahead, quad) + piece for piece in score_pieces()] + [("mt", ahead, quad)]


def attend(quad, others):
    steps, others = [], list(others)
    work = [s[6] if s[0] == "sa" else CH for s in others]
    total, whole = 0, sum((TT - kt) * P for kt in range(TT)) * QUAD * 0.85
    share, given = sum(work), 0
    for kt in range(TT):
        for h in range(QUAD):
            steps.append(("st", quad, kt, h))
            total += (TT - kt) * P
            while others and given < share * min(1.0, total / whole):
                steps.append(others.pop(0))
                given += work.pop(0)
            if kt and h == 1 and kt - 1 < TC:
                steps.append(("pv", quad, kt - 1, 0))
            if kt and h == 3:
                steps.append(("pv", quad, kt - 1, 1))
    return steps + others + [("pv", quad, TT - 1, 1)]


def project(first):
    a = [("xt", ch, c) for ch in range(NCH) for c in range(DT)]
    a += [("q", dt, ch) for dt in range(DT) for ch in range(NCH)]
    a += [("ckv", ch) for ch in range(NCH)]
    a += [("v", n) for n in range(TT // 2)]
    a += [("k", dt, ch) for dt in range(DT) for ch in range(NCH)]
    return [("ln1",)] + a if first else a


def down(ch):
    steps = []
    for t in range(TC + 1):
        steps += [("dn", ch, t)] if t < TC else []
        steps += [("fin", ch, t - 1)] if t else []
    return steps


def schedule(segment):
    if segment == "first":
        return ([("wq",)] + project(True) + [("mix",)]
                + [("wug", c, n) for c in range(DT) for n in range(2 * J // CH)]
                + [("wd", n) for n in range(JT // 2)] + maxima(1, 0))
    more = segment == "body"
    steps = []
    for quad in range(QUADS):
        if quad == QUADS - 1 and more:
            steps.append(("ln1",))
        steps += attend(quad, maxima(0, quad + 1) if quad < QUADS - 1 else [])
    a = project(False) if more else []
    for _ in range(8 if more else 0):
        steps.append(a.pop(0))
    for t in range(TT + 2):
        for tag, tile in (("ct", t), ("cn", t - 1), ("wo", t - 2)):
            if 0 <= tile < TT:
                steps.append((tag, tile))
        if t - 2 in (TC - 1, TT - 1):
            steps.append(("ln2", (t - 2) // TC))
        if a:
            steps.append(a.pop(0))
        if t == TT:
            steps += [("x2t", 0, c) for c in range(DT)]
    steps += a
    steps += [("gu", 0, jt) for jt in range(4)] + [("x2t", 1, c) for c in range(DT)]
    steps += [("gu", 0, jt) for jt in range(4, JT)]
    ahead = maxima(1, 0) if more else []
    per = -(-len(ahead) // (JT - 1))
    for jt in range(JT):
        steps.append(("gu", 1, jt))
        if jt == 0:
            steps += down(0)
        else:
            steps += ahead[:per]
            ahead = ahead[per:]
    return steps + down(1)


RING = {"st": "S", "sa": "X", "mt": "X", "xt": "X", "q": "X", "ckv": "X", "v": "X", "k": "X",
        "ct": "S", "cn": "X", "wo": "V", "x2t": "X", "gu": "S", "dn": "V", "wq": "X", "wug": "S",
        "wd": "V"}


class PsumTurns:

    def __init__(self):
        self.place, self.count = {}, {}
        for segment in ("first", "body", "last"):
            turn, count = {"S": 0, "V": 0, "X": 0}, {}
            for step in schedule(segment):
                if step[0] == "pv":
                    slot, step = f"V{step[3]}", ("pv", step[1], step[3])
                    if (segment, step) in self.place:
                        continue
                elif step[0] in RING:
                    ring = RING[step[0]]
                    slot = f"{ring}{turn[ring] % 2}"
                    turn[ring] += 1
                else:
                    continue
                self.place[segment, step] = slot, count.get(slot, 0)
                count[slot] = count.get(slot, 0) + 1
            self.count[segment] = count

    def of(self, segment, b, *step):
        slot, before = self.place[segment, step]
        if segment != "first":
            before = self.count["first"].get(slot, 0) + before + b * self.count["body"].get(slot, 0)
        return slot, before


LINKS = {"ln1": 1, "mix": 4, "mt": 2, "ct": 1, "wo": 1, "ln2": 3, "gu": 1, "dn": 1}


class Links:

    def __init__(self):
        self.total = {s: sum(LINKS.get(step[0], 0) for step in schedule(s)) for s in ("first", "body", "last")}
        self.now = 0

    def start(self, segment, b):
        assert segment == "first" or self.now == self.total[self.segment]
        self.segment, self.now = segment, 0
        self.base = 0 if segment == "first" else self.total["first"] + b * self.total["body"]

    def count(self):
        self.now += 1
        return self.base + self.now


def wait_past(engine, semaphore, count):
    if not (isinstance(count, int) and count == 0):
        engine.wait_ge(semaphore, count)


def layer(nc, x, w_dq, w_uq_t, w_dkv_t, w_uk_t, w_uv_t, w_o_t, b_o, su_ug, su_dp, wscale_ug,
          wscale_dp, w_up_t, w_gate_t, w_down_t, hadamard, identity, causal, out):
    turns = PsumTurns()
    links = Links()
    x_tiles = x.rearrange("b (t p) d -> b p t d", p=P)
    out_tiles = out.rearrange("b (t p) d -> b t p d", p=P)
    q_scratch = nc.dram_tensor("q_scratch", [3, H, DH, N], BF16, kind="Internal")
    k_scratch = nc.dram_tensor("k_scratch", [3, H, DH, N], BF16, kind="Internal")

    with ExitStack() as ctx:
        def sb(name, shape, dt=F32):
            return ctx.enter_context(nc.sbuf_tensor(name, shape, dt))

        def sem(name):
            return ctx.enter_context(nc.semaphore(name))

        psum = {}
        for ring, width in (("S", 2 * CH), ("V", CH), ("X", CH)):
            for i in range(2):
                psum[f"{ring}{i}"] = ctx.enter_context(nc.psum_tensor(f"psum_{ring}{i}", [P, width], F32))

        ident = sb("ident", [P, P])
        hada = sb("hada", [P, P])
        mask = sb("mask", [P, CH], BF16)
        wq = sb("wq", [P, DT, D])
        wdkv = sb("wdkv", [P, DT, P])
        wuk = sb("wuk", [P, D])
        wuv = sb("wuv", [P, D])
        wo = sb("wo", [P, DT, D])
        bo = sb("bo", [P, D])
        wug = sb("wug", [P, DT, 2 * J])
        wd = sb("wd", [P, JT, D])
        signs_ug = sb("signs_ug", [P, DT])
        signs_dp = sb("signs_dp", [P, JT])
        xa = sb("xa", [P, TT, D])
        xr = sb("xr", [P, TT, D])
        xT = sb("xT", [P, DT, N])
        ckvT = sb("ckvT", [P, N])
        parts = sb("parts", [P, 3, DT, N], BF16)
        rest = sb("rest", [P, 2, CH])
        q_stack = sb("q_stack", [P, H, N], BF16)
        k_stack = sb("k_stack", [P, H, N], BF16)
        v_ones = sb("v_ones", [P, TT, H * VW + 16])
        probs = sb("probs", [P, 2, QUAD, N])
        ctx_raw = sb("ctx_raw", [P, QUADS, N])
        ctx_n = sb("ctx_n", [P, 2, D])
        ctx_nT = sb("ctx_nT", [P, 2, D])
        row_max = sb("row_max", [P, QUAD, TT])
        row_max0 = sb("row_max0", [P, QUAD, TT - TC])
        max_rest = sb("max_rest", [QUAD * TT, P])
        max_parts = sb("max_parts", [QUAD * TT, 3, P], BF16)
        rden = sb("rden", [P, 2, H])
        norms = ("ln1", "lna", "lnx", "lnf")
        stats = {k: sb(f"stats_{k}", [P, TT, 6]) for k in norms}
        mv = {k: sb(f"mv_{k}", [P, TT, 2]) for k in norms}
        rstd = {k: sb(f"rstd_{k}", [P, TT]) for k in norms}
        var_eps = {k: sb(f"var_eps_{k}", [P, TT]) for k in norms}
        minus_half = sb("minus_half", [P, TT])
        hT = [probs[:, i].rearrange("p h n -> p (h n)").rearrange("p (j n) -> p j n", j=JT) for i in range(2)]
        y = probs[:, 1, 0:2, :].rearrange("p a n -> p (a n)").rearrange("p (t d) -> p t d", d=D)
        tanh_g = ctx_raw[:, 0, :].rearrange("p (i n) -> p i n", i=2)
        gated = ctx_raw[:, 1, :].rearrange("p (i n) -> p i n", i=2)
        ffn_n = ctx_raw[:, 2, 0:2 * D].rearrange("p (i n) -> p i n", i=2)
        w_raw = probs[:, 0].rearrange("p h n -> p (h n)").rearrange("p (c j) -> p c j", c=DT)
        w_mix = probs[:, 1].rearrange("p h n -> p (h n)").rearrange("p (c j) -> p c j", c=DT)
        d_mix = [ctx_raw[:, 2 * i:2 * i + 2, :].rearrange("p a n -> p (a n)") for i in range(2)]
        scale_ug = xr[:].rearrange("p t d -> p (t d)")
        scale_dp = ctx_nT[:, 0]
        w_dq_sb = q_stack[:, 0, :].bitcast(F32).rearrange("p (t c) -> p t c", t=DT)
        w_uq_sb = q_stack[:, 1, :].bitcast(F32).rearrange("p (t c) -> p t c", t=DT)

        psum_filled = {s: sem(f"psum_filled_{s}") for s in psum}
        psum_taken = {s: sem(f"psum_taken_{s}") for s in psum}
        proj_loaded = sem("proj_loaded")
        ffn_loaded = sem("ffn_loaded")
        xa_loaded = sem("xa_loaded")
        xr_loaded = sem("xr_loaded")
        out_stored = sem("out_stored")
        pads_ready = sem("pads_ready")
        w_mixed = sem("w_mixed")
        ln1_stats = sem("ln1_stats")
        var_ready = {k: sem(f"var_ready_{k}") for k in norms}
        ln1_rstd = sem("ln1_rstd")
        xn_ready = sem("xn_ready")
        part0_ready = sem("part0_ready")
        part1_ready = sem("part1_ready")
        part2_ready = sem("part2_ready")
        parts_stored = sem("parts_stored")
        stacks_loaded = sem("stacks_loaded")
        row_max_ready = sem("row_max_ready")
        max_parts_ready = sem("max_parts_ready")
        max_loaded = sem("max_loaded")
        masked = sem("masked")
        ln2_stats = sem("ln2_stats")
        ln2_rstd = sem("ln2_rstd")
        x2n_ready = sem("x2n_ready")
        tanh_ready = sem("tanh_ready")
        ln3_stats = sem("ln3_stats")
        ln3_rstd = sem("ln3_rstd")
        out_ready = sem("out_ready")
        dve_done = sem("dve_done")
        started = sem("started")

        block = ctx.enter_context(nc.Block())

        def segments(engine, emit):
            emit("first", -1)
            with engine.Fori(0, B - 1) as b:
                emit("body", b)
            emit("last", B - 1)

        def wait_apart(engine, semaphore, count):
            if not isinstance(count, int):
                engine.compute_val(count)
            engine.wait_ge(started, 1)
            engine.wait_ge(semaphore, count)

        def chunk(ch):
            return slice(CH * ch, CH * (ch + 1))

        @block.sync
        def _(sp):
            sp.dma_start(xa[:], x_tiles[0]).then_inc(xa_loaded, 16)
            sp.dma_start(w_dq_sb, w_dq.rearrange("(t p) c -> p t c", p=P)).then_inc(proj_loaded, 16)
            sp.dma_start(w_uq_sb, w_uq_t.rearrange("(t p) c -> p t c", p=P)).then_inc(proj_loaded, 16)
            sp.dma_start(ident[:], identity).then_inc(proj_loaded, 16)
            sp.wait_ge(pads_ready, 1)
            sp.dma_start(wdkv[:, :, 0:CKV], w_dkv_t.rearrange("(t p) c -> p t c", p=P)).then_inc(proj_loaded, 16)
            sp.dma_start(wuk[0:CKV, :], w_uk_t).then_inc(proj_loaded, 16)
            sp.dma_start(wuv[0:CKV, :], w_uv_t).then_inc(proj_loaded, 16)
            for dst, src in (
                (w_raw[:, :, 0:J], w_up_t.rearrange("(t p) j -> p t j", p=P)),
                (w_raw[:, :, J:2 * J], w_gate_t.rearrange("(t p) j -> p t j", p=P)),
                (d_mix[0].rearrange("p (t c) -> p t c", c=D), w_down_t.rearrange("(t p) c -> p t c", p=P)),
                (hada[:], hadamard), (mask[:], causal),
                (signs_ug[:], su_ug),
                (signs_dp[:], su_dp),
                (scale_ug, wscale_ug.partition_broadcast(P)), (scale_dp, wscale_dp.partition_broadcast(P)),
                (bo[:], b_o.partition_broadcast(P)), (wo[:], w_o_t.rearrange("(t p) c -> p t c", p=P)),
            ):
                sp.dma_start(dst, src).then_inc(ffn_loaded, 16)

            def restack(i, which):
                scratch = (q_scratch, k_scratch)[which]
                stack = (q_stack, k_stack)[which]
                wait_apart(sp, part2_ready, 8 * i + 4 * which + 4)
                if not (isinstance(i, int) and i == 0):
                    wait_apart(sp, stacks_loaded, 16 * 12 * i)
                for s in range(3):
                    sp.dma_start(scratch[s].rearrange("(t h) p n -> (h p) t n", t=DT), parts[:, s])\
                      .then_inc(parts_stored, 16)
                sp.wait_ge(parts_stored, 48 * (2 * i + which + 1))
                for s, pair in enumerate(STRIPS):
                    sp.dma_start(stack[DH * s:DH * (s + 1)], scratch[pair[which]].rearrange("h p n -> p h n"))\
                      .then_inc(stacks_loaded, 16)

            def emit(segment, b):
                for step in schedule(segment):
                    kind = step[0]
                    if kind in ("q", "k") and step[1:] == (DT - 1, NCH - 1):
                        restack(b + 1, 0 if kind == "q" else 1)
                    if kind == "mt":
                        _, ahead, quad = step
                        sp.wait_ge(max_parts_ready, QUADS * (b + ahead) + quad + 1)
                        for j in range(3):
                            row = q_stack[KS + j:KS + j + 1, QUAD * quad:QUAD * (quad + 1), :]
                            sp.dma_start(row.rearrange("o h (t n) -> o (h t) n", n=P), max_parts[:, j, :])\
                              .then_inc(max_loaded, 16)
                    if step == ("st", 0, 0, 0) and segment == "body":
                        slot, before = turns.of(segment, b, *step)
                        wait_apart(sp, psum_filled[slot], before + 1)
                        sp.dma_start(xa[:], x_tiles[b + 1]).then_inc(xa_loaded, 16)
                    if kind == "fin":
                        t = TC * step[1] + step[2]
                        wait_apart(sp, out_ready, b * TT + t + 1)
                        sp.dma_start(out_tiles[b, t], xr[:, t, :]).then_inc(out_stored, 16)
                if segment == "first":
                    for n in (2 * J // CH - 2, 2 * J // CH - 1):
                        slot, before = turns.of(segment, b, "wug", DT - 1, n)
                        sp.wait_ge(psum_taken[slot], before + 1)
                    sp.dma_start(xr[:], x_tiles[0]).then_inc(xr_loaded, 16)
                if segment == "body":
                    wait_apart(sp, out_stored, 16 * TT * (b + 1))
                    sp.dma_start(xr[:], x_tiles[b + 1]).then_inc(xr_loaded, 16)

            segments(sp, emit)
            sp.wait_ge(out_stored, 16 * TT * B)

        @block.gpsimd
        def _(pool):
            nc.gpsimd.memset(minus_half[:], -0.5).then_inc(started, 1)
            nc.gpsimd.memset(wdkv[:], 0.0)
            nc.gpsimd.memset(wuk[:], 0.0)
            nc.gpsimd.memset(wuv[:], 0.0).then_inc(pads_ready, 1)
            nc.gpsimd.memset(v_ones[:, :, H * VW:], 0.0)
            nc.gpsimd.memset(v_ones[:, :, 0:H * VW].rearrange("p t (h w) -> p t h w", w=VW)[:, :, :, DH:VW], 1.0)\
              .then_inc(pads_ready, 1)

            def root(key, rows, n, done):
                nc.gpsimd.tensor_scalar(var_eps[key][:, rows], mv[key][:, rows, 1], EPS, None, ALU.add)\
                  .then_inc(var_ready[key], 1)
                pool.wait_ge(var_ready[key], n)
                nc.gpsimd.tensor_tensor(rstd[key][:, rows], var_eps[key][:, rows], minus_half[:, rows], ALU.pow)\
                  .then_inc(done, 1)

            pool.wait_ge(pads_ready, 2)

            def emit(segment, b):
                splits = 0
                for step in schedule(segment):
                    kind = step[0]
                    if kind == "ln1":
                        wait_apart(pool, ln1_stats, b + 2)
                        root("ln1", slice(0, TT), b + 2, ln1_rstd)
                    if kind == "mix":
                        pool.wait_ge(part2_ready, 8)
                        nc.gpsimd.memset(k_stack[KS:P], 1.0).then_inc(pads_ready, 1)
                        pool.wait_ge(pads_ready, 3)
                    if kind in ("q", "k"):
                        _, dt, ch = step
                        pool.wait_ge(part1_ready, 8 * (b + 1) + splits + 1)
                        nc.gpsimd.tensor_tensor(parts[:, 2, dt, chunk(ch)], rest[:, splits % 2],
                                                parts[:, 1, dt, chunk(ch)], ALU.subtract).then_inc(part2_ready, 1)
                        splits += 1
                    if kind == "st":
                        _, quad, kt, h = step
                        slot, before = turns.of(segment, b, *step)
                        wait_apart(pool, psum_taken[slot], before + 1)
                        tile = probs[:, kt % 2, h, kt * P:(kt + 1) * P]
                        nc.gpsimd.affine_select(out=tile, in_=tile, compare_op=ALU.is_ge, fill=0.0, base=0,
                                                pattern=[[1, P]], channel_multiplier=-1).then_inc(masked, 1)
                    if kind == "ln2":
                        ch = step[1]
                        for n, key in enumerate(("lna", "lnx")):
                            wait_apart(pool, ln2_stats, b * 2 * NCH + 2 * ch + n + 1)
                            root(key, slice(TC * ch, TC * (ch + 1)), b * NCH + ch + 1, ln2_rstd)
                    if kind == "dn":
                        t = TC * step[1] + step[2]
                        wait_apart(pool, ln3_stats, b * TT + t + 1)
                        root("lnf", slice(t, t + 1), b * TT + t + 1, ln3_rstd)

            segments(pool, emit)

        @block.scalar
        def _(act):
            def emit(segment, b):
                splits = 0
                for step in schedule(segment):
                    kind = step[0]
                    if kind in ("wq", "xt", "x2t", "q", "k", "ckv", "v", "st", "cn", "gu"):
                        slot, before = turns.of(segment, b, *step)
                        src = psum[slot]
                    if kind in ("q", "k") and splits % 4 == 0:
                        wait_past(act, parts_stored, 48 * (2 * (b + 1) + splits // 4))
                    if kind in ("wq", "xt", "x2t", "q", "k", "ckv", "v", "st", "cn", "gu"):
                        act.wait_ge(psum_filled[slot], before + 1)
                    if kind == "wq":
                        nc.scalar.activation(wq[:].rearrange("p c d -> p (c d)"), src[:], ACT.Copy)\
                          .then_inc(psum_taken[slot], 1)
                    if kind in ("xt", "x2t"):
                        _, ch, c = step
                        nc.scalar.activation(xT[:, c, chunk(ch)], src[:], ACT.Copy).then_inc(psum_taken[slot], 1)
                    if kind in ("q", "k"):
                        _, dt, ch = step
                        nc.scalar.activation(parts[:, 0, dt, chunk(ch)], src[:], ACT.Copy).then_inc(part0_ready, 1)
                        splits += 1
                    if kind == "ckv":
                        nc.scalar.activation(ckvT[:, chunk(step[1])], src[:], ACT.Copy).then_inc(psum_taken[slot], 1)
                    if kind == "v":
                        n = step[1]
                        dst = v_ones[:, 2 * n:2 * n + 2, 0:H * VW].rearrange("p t (h w) -> p t h w", w=VW)
                        nc.scalar.activation(dst[:, :, :, 0:DH], src[:].rearrange("p (t h w) -> p t h w", t=2, w=DH),
                                             ACT.Copy).then_inc(psum_taken[slot], 1)
                    if kind == "st":
                        _, quad, kt, h = step
                        nc.scalar.activation(probs[:, kt % 2, h, kt * P:], src[:, kt * P:], ACT.Exp,
                                             scale=DH ** -0.5).then_inc(psum_taken[slot], 1)
                    if kind == "pv" and (step[2], step[3]) in ((TC - 1, 0), (TT - 1, 1)):
                        _, quad, _, half = step
                        slot, before = turns.of(segment, b, "pv", quad, half)
                        act.wait_ge(psum_filled[slot], before + 1)
                        nc.scalar.activation(ctx_raw[:, quad, chunk(half)], psum[slot][:], ACT.Copy)\
                          .then_inc(psum_taken[slot], 1)
                    if kind == "cn":
                        nc.scalar.activation(ctx_nT[:, step[1] % 2], src[:, 0:D], ACT.Copy)\
                          .then_inc(psum_taken[slot], 1)
                    if kind == "gu":
                        nc.scalar.activation(tanh_g[:, step[2] % 2], src[:, 0:CH], ACT.Tanh, scale=0.5)\
                          .then_inc(tanh_ready, 1)

            segments(act, emit)

        @block.vector
        def _(dve):
            def moments(key, tile, source):
                return nc.vector.bn_stats(stats[key][:, tile, :], source)

            def aggregate(key, tile):
                return nc.vector.bn_aggr(mv[key][:, tile, :], stats[key][:, tile, :])

            def normalise(dst, source, key, t):
                return nc.vector.tensor_scalar(dst, source, mv[key][:, t, 0:1], rstd[key][:, t:t + 1],
                                               ALU.subtract, ALU.mult)

            def emit(segment, b):
                links.start(segment, b)
                splits = 0
                for step in schedule(segment):
                    kind = step[0]
                    if kind in ("sa", "mt", "q", "k", "ct", "wo", "gu", "dn", "wug", "wd"):
                        slot, before = turns.of(segment, b, *step)
                        src = psum[slot]
                        if kind == "sa":
                            wait_apart(dve, psum_filled[slot], before + 1)
                        elif kind not in ("mt", "q", "k"):
                            dve.wait_ge(psum_filled[slot], before + 1)
                    if kind == "sa":
                        _, _, quad, h, qt, k0, keys = step
                        if k0 + keys < (qt + 1) * P:
                            nc.vector.tensor_reduce(row_max0[:, h, qt - TC:qt - TC + 1], src[:, 0:keys], AX_X, ALU.max)\
                              .then_inc(psum_taken[slot], 1)
                        else:
                            nc.vector.tensor_tensor_reduce(src[:, 0:keys], src[:, 0:keys], mask[:, CH - keys:CH],
                                                           1.0, MASKED, ALU.add, ALU.max,
                                                           row_max[:, h, qt:qt + 1]).then_inc(psum_taken[slot], 1)
                            last_piece = slot, before
                    if kind == "mt":
                        _, ahead, quad = step
                        dve.wait_ge(psum_taken[last_piece[0]], last_piece[1] + 1)
                        nc.vector.tensor_tensor(row_max[:, :, TC:TT], row_max[:, :, TC:TT], row_max0[:], ALU.max)\
                          .then_inc(row_max_ready, 1)
                        dve.wait_ge(psum_filled[slot], before + 1)
                        wait_past(dve, max_loaded, 48 * (QUADS * (b + ahead) + quad))
                        done = links.count()
                        nc.vector.tensor_scalar(max_parts[:, 0, :], src[0:QUAD * TT, 0:P], -1.0, None, ALU.mult)\
                          .then_inc(dve_done, 1)
                        dve.wait_ge(dve_done, done)
                        done = links.count()
                        nc.vector.scalar_tensor_tensor(out=max_rest[:], in0=src[0:QUAD * TT, 0:P], scalar=-1.0,
                                                       in1=max_parts[:, 0, :], op0=ALU.mult, op1=ALU.subtract)\
                          .then_inc(psum_taken[slot], 1)
                        dve.wait_ge(psum_taken[slot], before + 1)
                        nc.vector.tensor_copy(max_parts[:, 1, :], max_rest[:]).then_inc(dve_done, 1)
                        dve.wait_ge(dve_done, done)
                        nc.vector.tensor_tensor(max_parts[:, 2, :], max_rest[:], max_parts[:, 1, :], ALU.subtract)\
                          .then_inc(max_parts_ready, 1)
                    if kind == "ln1":
                        dve.wait_ge(xa_loaded, 16 * (b + 2))
                        for t in range(TT):
                            last = moments("ln1", t, xa[:, t, :])
                        done = links.count()
                        last.then_inc(dve_done, 1)
                        wait_apart(dve, dve_done, done)
                        for t in range(TT):
                            last = aggregate("ln1", t)
                        last.then_inc(ln1_stats, 1)
                        dve.wait_ge(ln1_stats, b + 2)
                        dve.wait_ge(ln1_rstd, b + 2)
                        for t in range(TT):
                            last = normalise(xa[:, t, :], xa[:, t, :], "ln1", t)
                        last.then_inc(xn_ready, 1)
                    if kind in ("q", "k"):
                        _, dt, ch = step
                        n = 8 * (b + 1) + splits
                        if splits > 1:
                            dve.wait_ge(part2_ready, n - 1)
                        dve.wait_ge(part0_ready, n + 1)
                        nc.vector.tensor_tensor(rest[:, splits % 2], src[:], parts[:, 0, dt, chunk(ch)], ALU.subtract)\
                          .then_inc(psum_taken[slot], 1)
                        dve.wait_ge(psum_taken[slot], before + 1)
                        nc.vector.tensor_copy(parts[:, 1, dt, chunk(ch)], rest[:, splits % 2])\
                          .then_inc(part1_ready, 1)
                        splits += 1
                    if kind == "ct":
                        t = step[1]
                        heads = src[:, 0:CH].rearrange("p (h w) -> p h w", h=H)
                        done = links.count()
                        nc.vector.reciprocal(rden[:, t % 2, :], heads[:, :, DH]).then_inc(dve_done, 1)
                        dve.wait_ge(dve_done, done)
                        if t > 1:
                            other, uses = turns.of(segment, b, "cn", t - 2)
                            dve.wait_ge(psum_filled[other], uses + 1)
                        nc.vector.tensor_tensor(ctx_n[:, t % 2].rearrange("p (h w) -> p h w", h=H), heads[:, :, 0:DH],
                                                rden[:, t % 2, :].unsqueeze(2).broadcast_to((P, H, DH)), ALU.mult)\
                          .then_inc(psum_taken[slot], 1)
                    if kind == "wo":
                        t = step[1]
                        nc.vector.tensor_tensor(y[:, t, :], src[:, 0:D], bo[:], ALU.add).then_inc(psum_taken[slot], 1)
                        dve.wait_ge(psum_taken[slot], before + 1)
                        done = links.count()
                        moments("lna", t, y[:, t, :]).then_inc(dve_done, 1)
                    if kind == "ln2":
                        ch = step[1]
                        tiles = range(TC * ch, TC * (ch + 1))
                        before = b * 2 * NCH + 2 * ch
                        wait_apart(dve, dve_done, done)
                        for t in tiles:
                            last = aggregate("lna", t)
                        last.then_inc(ln2_stats, 1)
                        dve.wait_ge(ln2_stats, before + 1)
                        dve.wait_ge(ln2_rstd, before + 1)
                        for t in tiles:
                            last = normalise(y[:, t, :], y[:, t, :], "lna", t)
                        done = links.count()
                        last.then_inc(dve_done, 1)
                        dve.wait_ge(dve_done, done)
                        dve.wait_ge(xr_loaded, 16 * (b + 1))
                        for t in tiles:
                            last = nc.vector.tensor_tensor(xr[:, t, :], xr[:, t, :], y[:, t, :], ALU.add)
                        done = links.count()
                        last.then_inc(dve_done, 1)
                        dve.wait_ge(dve_done, done)
                        for t in tiles:
                            last = moments("lnx", t, xr[:, t, :])
                        done = links.count()
                        last.then_inc(dve_done, 1)
                        wait_apart(dve, dve_done, done)
                        for t in tiles:
                            last = aggregate("lnx", t)
                        last.then_inc(ln2_stats, 1)
                        dve.wait_ge(ln2_stats, before + 2)
                        dve.wait_ge(ln2_rstd, before + 2)
                        for t in tiles:
                            last = normalise(y[:, t, :], xr[:, t, :], "lnx", t)
                        last.then_inc(x2n_ready, 1)
                    if kind == "gu":
                        _, ch, jt = step
                        dve.wait_ge(tanh_ready, b * NCH * JT + JT * ch + jt + 1)
                        done = links.count()
                        nc.vector.scalar_tensor_tensor(out=gated[:, jt % 2], in0=tanh_g[:, jt % 2], scalar=1.0,
                                                       in1=src[:, 0:CH], op0=ALU.add, op1=ALU.mult)\
                          .then_inc(dve_done, 1)
                        dve.wait_ge(dve_done, done)
                        nc.vector.tensor_tensor(hT[ch][:, jt, :], gated[:, jt % 2], src[:, CH:2 * CH], ALU.mult)\
                          .then_inc(psum_taken[slot], 1)
                    if kind == "dn":
                        t = TC * step[1] + step[2]
                        done = links.count()
                        moments("lnf", t, src[:, 0:D]).then_inc(dve_done, 1)
                        wait_apart(dve, dve_done, done)
                        aggregate("lnf", t).then_inc(ln3_stats, 1)
                    if kind == "fin":
                        t = TC * step[1] + step[2]
                        slot, before = turns.of(segment, b, "dn", *step[1:])
                        dve.wait_ge(ln3_stats, b * TT + t + 1)
                        dve.wait_ge(ln3_rstd, b * TT + t + 1)
                        normalise(ffn_n[:, t % 2], psum[slot][:, 0:D], "lnf", t).then_inc(psum_taken[slot], 1)
                        dve.wait_ge(psum_taken[slot], before + 1)
                        nc.vector.tensor_tensor(xr[:, t, :], xr[:, t, :], ffn_n[:, t % 2], ALU.add)\
                          .then_inc(out_ready, 1)
                    if kind == "mix":
                        dve.wait_ge(ffn_loaded, 16 * 11)
                        nc.vector.tensor_tensor(w_mix[:, 0], w_raw[:, 0], w_raw[:, 1], ALU.add)
                        nc.vector.tensor_tensor(w_mix[:, 1], w_raw[:, 0], w_raw[:, 1], ALU.subtract)
                        nc.vector.tensor_scalar(signs_ug[:], signs_ug[:], D ** -0.5, None, ALU.mult)
                        done = links.count()
                        nc.vector.tensor_scalar(signs_dp[:], signs_dp[:], 0.5 * J ** -0.5, None, ALU.mult)\
                          .then_inc(dve_done, 1)
                        for stage in range(3):
                            a, z = (m.rearrange("p (o two s) -> p o two s", two=2, s=D << stage)
                                    for m in (d_mix[stage % 2], d_mix[1 - stage % 2]))
                            dve.wait_ge(dve_done, done)
                            nc.vector.tensor_tensor(z[:, :, 0], a[:, :, 0], a[:, :, 1], ALU.add)
                            last = nc.vector.tensor_tensor(z[:, :, 1], a[:, :, 0], a[:, :, 1], ALU.subtract)
                            done = links.count()
                            last.then_inc(dve_done, 1)
                        dve.wait_ge(dve_done, done)
                    if kind == "wug":
                        _, c, n = step
                        nc.vector.scalar_tensor_tensor(out=wug[:, c, chunk(n)], in0=src[:, 0:CH], scalar=signs_ug[:, c:c + 1],
                                                       in1=scale_ug[:, chunk(n)], op0=ALU.mult, op1=ALU.mult)\
                          .then_inc(psum_taken[slot], 1)
                    if kind == "wd":
                        for i in range(2):
                            jt = 2 * step[1] + i
                            last = nc.vector.scalar_tensor_tensor(
                                out=wd[:, jt, :], in0=src[:, D * i:D * (i + 1)], scalar=signs_dp[:, jt:jt + 1],
                                in1=scale_dp, op0=ALU.mult, op1=ALU.mult)
                        last.then_inc(psum_taken[slot], 1)

            dve.wait_ge(ffn_loaded, 16 * 11)
            segments(dve, emit)

        @block.tensor
        def _(pe):
            def emit(segment, b):
                for step in schedule(segment):
                    kind = step[0]
                    if kind in RING:
                        slot, before = turns.of(segment, b, *step)
                        dst = psum[slot]
                        if kind != "mt":
                            wait_past(pe, psum_taken[slot], before)
                    if kind == "wq":
                        pe.wait_ge(proj_loaded, 16 * 6)
                        for ct in range(DT):
                            for t in range(DT):
                                last = nc.tensor.matmul(dst[:, D * ct:D * (ct + 1)], w_dq_sb[:, t, P * ct:P * (ct + 1)],
                                                        w_uq_sb[:, t, :], start=(t == 0), stop=(t == DT - 1))
                        last.then_inc(psum_filled[slot], 1)
                    if kind == "xt":
                        _, ch, c = step
                        pe.wait_ge(xn_ready, b + 2)
                        for t in range(TC):
                            last = nc.tensor.transpose(dst[:, P * t:P * (t + 1)],
                                                       xa[:, TC * ch + t, P * c:P * (c + 1)], ident[:])
                        last.then_inc(psum_filled[slot], 1)
                    if kind in ("q", "ckv"):
                        dt, ch = (step[1], step[2]) if kind == "q" else (0, step[1])
                        for c in range(DT):
                            wait_taken(segment, b, "xt", ch, c)
                        if (kind, dt, ch) == ("q", 0, 0) and segment == "first":
                            wait_taken(segment, b, "wq")
                        for c in range(DT):
                            w = wq[:, c, P * dt:P * (dt + 1)] if kind == "q" else wdkv[:, c, :]
                            last = nc.tensor.matmul(dst[:], w, xT[:, c, chunk(ch)], start=(c == 0), stop=(c == DT - 1))
                        last.then_inc(psum_filled[slot], 1)
                    if kind == "v":
                        n = step[1]
                        wait_taken(segment, b, "ckv", 2 * n // TC)
                        for i in range(2):
                            t = 2 * n + i
                            last = nc.tensor.matmul(dst[:, D * i:D * (i + 1)], ckvT[:, P * t:P * (t + 1)], wuv[:],
                                                    start=True, stop=True)
                        last.then_inc(psum_filled[slot], 1)
                    if kind == "k":
                        _, dt, ch = step
                        wait_taken(segment, b, "ckv", ch)
                        nc.tensor.matmul(dst[:], wuk[:, P * dt:P * (dt + 1)], ckvT[:, chunk(ch)], start=True, stop=True)\
                          .then_inc(psum_filled[slot], 1)
                    if kind == "sa":
                        _, ahead, quad, h, qt, k0, keys = step
                        head = QUAD * quad + h
                        if (quad, h, qt, k0) == (0, 0, 0, 0):
                            pe.wait_ge(stacks_loaded, 16 * 12 * (b + ahead + 1))
                        nc.tensor.matmul(dst[:, 0:keys], q_stack[0:KS, head, P * qt:P * (qt + 1)],
                                         k_stack[0:KS, head, k0:k0 + keys], start=True, stop=True)\
                          .then_inc(psum_filled[slot], 1)
                    if kind == "mt":
                        _, ahead, quad = step
                        pe.wait_ge(row_max_ready, QUADS * (b + ahead) + quad + 1)
                        wait_past(pe, psum_taken[slot], before)
                        nc.tensor.transpose(dst[0:QUAD * TT, 0:P], row_max[:].rearrange("p h t -> p (h t)"), ident[:])\
                          .then_inc(psum_filled[slot], 1)
                    if kind == "st":
                        _, quad, kt, h = step
                        head = QUAD * quad + h
                        if (kt, h) == (0, 0):
                            pe.wait_ge(max_loaded, 48 * (QUADS * b + quad + 1))
                        for q0 in range(kt * P // CH * CH, N, CH):
                            cols = slice(max(q0, kt * P), q0 + CH)
                            last = nc.tensor.matmul(dst[:, cols], k_stack[0:KM, head, P * kt:P * (kt + 1)],
                                                    q_stack[0:KM, head, cols], start=True, stop=True)
                        last.then_inc(psum_filled[slot], 1)
                    if kind == "pv":
                        _, quad, kt, half = step
                        slot, before = turns.of(segment, b, "pv", quad, half)
                        if kt == 0:
                            wait_past(pe, psum_taken[slot], before)
                        pe.wait_ge(masked, (b * QUADS + quad) * QUAD * TT + QUAD * (kt + 1))
                        q0 = max(CH * half, kt * P)
                        ends = kt == (TC, TT)[half] - 1
                        for h in range(QUAD):
                            col = VW * (QUAD * quad + h)
                            last = nc.tensor.matmul(psum[slot][32 * h:32 * (h + 1), q0 - CH * half:CH],
                                                    v_ones[:, kt, col:col + 32], probs[:, kt % 2, h, q0:CH * (half + 1)],
                                                    start=(kt == 0), stop=ends, skip_group_check=True)
                        if ends:
                            last.then_inc(psum_filled[slot], 1)
                    if kind == "ct":
                        t = step[1]
                        if t == 0:
                            for half in range(2):
                                wait_taken(segment, b, "pv", QUADS - 1, half)
                        for quad in range(QUADS):
                            last = nc.tensor.transpose(dst[:, P * quad:P * (quad + 1)],
                                                       ctx_raw[:, quad, P * t:P * (t + 1)], ident[:])
                        last.then_inc(psum_filled[slot], 1)
                    if kind == "cn":
                        t = step[1]
                        wait_taken(segment, b, "ct", t)
                        for c in range(DT):
                            last = nc.tensor.transpose(dst[:, P * c:P * (c + 1)], ctx_n[:, t % 2, P * c:P * (c + 1)],
                                                       ident[:])
                        last.then_inc(psum_filled[slot], 1)
                    if kind == "wo":
                        t = step[1]
                        wait_taken(segment, b, "cn", t)
                        for c in range(DT):
                            last = nc.tensor.matmul(dst[:, 0:D], ctx_nT[:, t % 2, P * c:P * (c + 1)], wo[:, c, :],
                                                    start=(c == 0), stop=(c == DT - 1))
                        last.then_inc(psum_filled[slot], 1)
                    if kind == "x2t":
                        _, ch, c = step
                        pe.wait_ge(x2n_ready, b * NCH + ch + 1)
                        for t in range(TC):
                            last = nc.tensor.transpose(dst[:, P * t:P * (t + 1)], y[:, TC * ch + t, P * c:P * (c + 1)],
                                                       ident[:])
                        last.then_inc(psum_filled[slot], 1)
                    if kind == "gu":
                        _, ch, jt = step
                        for c in range(DT):
                            wait_taken(segment, b, "x2t", ch, c)
                        for i, j0 in enumerate((J, 0)):
                            for c in range(DT):
                                last = nc.tensor.matmul(dst[:, CH * i:CH * (i + 1)],
                                                        wug[:, c, j0 + P * jt:j0 + P * (jt + 1)], xT[:, c, chunk(ch)],
                                                        start=(c == 0), stop=(c == DT - 1))
                        last.then_inc(psum_filled[slot], 1)
                    if kind == "dn":
                        _, ch, t = step
                        wait_taken(segment, b, "gu", ch, JT - 1)
                        for jt in range(JT):
                            last = nc.tensor.matmul(dst[:, 0:D], hT[ch][:, jt, P * t:P * (t + 1)], wd[:, jt, :],
                                                    start=(jt == 0), stop=(jt == JT - 1))
                        last.then_inc(psum_filled[slot], 1)
                    if kind in ("wug", "wd"):
                        if step == ("wug", 0, 0):
                            pe.wait_ge(dve_done, LINKS["ln1"] + LINKS["mix"])
                            pe.wait_ge(ffn_loaded, 16 * 11)
                        rhs = w_mix[:, step[1], chunk(step[2])] if kind == "wug" else d_mix[1][:, chunk(step[1])]
                        nc.tensor.matmul(dst[:, 0:CH], hada[:], rhs, start=True, stop=True).then_inc(psum_filled[slot], 1)
                if segment == "first":
                    wait_taken(segment, b, "wd", JT // 2 - 1)
                    pe.wait_ge(pads_ready, 3)

            def wait_taken(segment, b, *step):
                slot, before = turns.of(segment, b, *step)
                pe.wait_ge(psum_taken[slot], before + 1)

            segments(pe, emit)



def kernel(**inputs):
    import numpy as np
    import concourse.bacc as bacc
    from concourse.bass_utils import run_bass_kernel_spmd

    a = {k[3:]: np.asarray(v) for k, v in inputs.items()}
    sylvester = np.ones((1, 1), np.float32)
    while len(sylvester) < P:
        sylvester = np.block([[sylvester, sylvester], [sylvester, -sylvester]])
    bf16 = mybir.dt.np(BF16)
    causal = np.zeros((P, CH), np.float32)
    causal[:, CH - P:] = np.where(np.arange(P)[None, :] > np.arange(P)[:, None], MASKED, 0.0)
    arrays = {
        "x": a["attn_x"], "w_dq": a["attn_W_DQ"], "w_uq_t": a["attn_W_UQ"].T, "w_dkv_t": a["attn_W_DKV"].T,
        "w_uk_t": a["attn_W_UK"].T, "w_uv_t": a["attn_W_UV"].T, "w_o_t": a["attn_W_O"].T, "b_o": a["attn_b_O"],
        "su_ug": a["ffn_SU_ug"].reshape(DT, P).T, "su_dp": a["ffn_SU_dp"].reshape(JT, P).T, "wscale_ug": a["ffn_Wscale_ug"],
        "wscale_dp": a["ffn_Wscale_dp"], "w_up_t": a["ffn_W_up"].T, "w_gate_t": a["ffn_W_gate"].T,
        "w_down_t": a["ffn_W_down"].T, "hadamard": sylvester, "identity": np.eye(P, dtype=np.float32),
        "causal": causal.astype(bf16),
    }
    arrays = {k: np.ascontiguousarray(v) for k, v in arrays.items()}
    nc = bacc.Bacc("TRN2", target_bir_lowering=False, num_devices=1)
    args = [nc.dram_tensor(k, v.shape, mybir.dt.from_np(v.dtype), kind="ExternalInput").ap()
            for k, v in arrays.items()]
    args.append(nc.dram_tensor("out", (B, N, D), F32, kind="ExternalOutput").ap())
    layer(nc, *args)
    result = run_bass_kernel_spmd(nc, [arrays], core_ids=[0])
    return result.results[0]["out"]
```

```python
from contextlib import ExitStack

import concourse.bass as bass
from concourse import mybir

P = 128
B, N, D = 4, 1024, 256
H, DH = 16, 16
CKV = 64
J = 1024
TT = N // P
CH = 512
NCH = N // CH
TC = CH // P
DT = D // P
JT = J // P
QUAD = 4
QUADS = H // QUAD
VW = DH + 1
STRIPS = [(0, 0), (0, 1), (0, 2), (1, 0), (1, 1), (2, 0)]
KS = len(STRIPS) * DH
KM = KS + 3
SA_END, PROJECT_START = 0.70, 0.72
ROOT_STEPS = {"ln1": 2, "lna": 4, "lnx": 4, "lnf": 4}
AHEAD = 2
PARTS = 4
LAST_KEYS = (3, 4)
KEY_TILES = [0, 7, 1, 6, 2, 5, 3, 4]
EPS = 1e-5
MASKED = -3.0e38

F32 = mybir.dt.float32
BF16 = mybir.dt.bfloat16
ALU = mybir.AluOpType
ACT = mybir.ActivationFunctionType
AX_X = mybir.AxisListType.X



def score_pieces():
    return [(h, qt, k0, min((qt + 1) * P - k0, CH))
            for h in range(QUAD) for qt in range(TT) for k0 in range(0, (qt + 1) * P, CH)]


def maxima(ahead, quad):
    return [("sa", ahead, quad) + piece for piece in score_pieces()] + [("mt", ahead, quad)]


def work(step):
    kind = step[0]
    if kind == "sa":
        return 0.42 * step[6], [("DVE", 70 + 1.04 * step[6])]
    if kind == "st":
        keys = (TT - step[2]) * P
        mask = [("Pool", 600)] if step[3] == QUAD - 1 else []
        return 0.42 * keys, [("ACT", 60 + 0.84 * keys)] + mask
    if kind == "pv":
        copy = [("ACT", 480)] if step[2] == LAST_KEYS[step[3]] else []
        return 1.83 * (CH * (step[3] + 1) - max(CH * step[3], step[2] * P)), copy
    if kind in ("gu", "dn") and not ends(step):
        return 860, []
    if kind == "ln2":
        return 0, ([("DVE", 400), ("Pool", 1900)], [("DVE", 3200), ("Pool", 1900)], [("ACT", 1800)])[step[2]]
    return {
        "gu": (860, [("ACT", 480), ("DVE", 1300)]), "dn": (860, [("ACT", 270), ("DVE", 550), ("Pool", 1500)]),
        "fin": (0, [("ACT", 450), ("Pool", 650)]), "q": (1720, [("ACT", 480), ("DVE", 1050)]),
        "k": (860, [("ACT", 480), ("DVE", 1050)]), "ckv": (1720, [("ACT", 480)]), "v": (860, [("ACT", 480)]),
        "xt": (860, [("ACT", 480)]), "x2t": (860, [("ACT", 480)]), "ln1": (0, [("DVE", 7000)]),
        "ct": (430, [("DVE", 650)]), "cn": (215, [("ACT", 270)]), "wo": (860, [("DVE", 700)]),
        "mt": (200, [("DVE", 1500)]), "stack": (0, []),
    }[kind]


def needs(step):
    kind = step[0]
    if kind == "st" and step[2:] == (KEY_TILES[0], 0) and step[1] >= AHEAD:
        return [("mt", 0, step[1])]
    if kind == "pv":
        return [("st", step[1], step[2], QUAD - 1)]
    if kind == "sa" and step[1]:
        return [("stack",)]
    if kind in ("q", "ckv"):
        return [("xt", step[-1], c) for c in range(DT)]
    if kind in ("k", "v"):
        return [("ckv", step[-1] if kind == "k" else 2 * step[1] // TC)]
    if kind == "stack":
        return [("k", DT - 1, NCH - 1), ("st", QUADS - 1, KEY_TILES[-1], QUAD - 1)]
    if kind == "ln2":
        return [("wo", TC * step[1] + TC - 1) if step[2] == 0 else ("ln2", step[1], step[2] - 1)]
    if kind == "gu":
        return [("x2t", step[1], c) for c in range(DT)]
    return {
        "xt": [("ln1",)], "ct": [("pv", QUADS - 1, LAST_KEYS[half], half) for half in range(2)],
        "cn": [("ct", step[-1])], "wo": [("cn", step[-1])], "x2t": [("ln2", step[1], 2)] if len(step) > 2 else [],
        "dn": [("gu", step[1], JT - 1)] if len(step) > 2 else [], "fin": [("dn",) + step[1:]],
    }.get(kind, [])


LATENCY = 140
DMA_TIME = {"mt": 4000, "stack": 14000}


class Merge:

    def __init__(self):
        self.free = {"PE": 0, "ACT": 0, "DVE": 0, "Pool": 0}
        self.slots = {ring: [0, 0] for ring in "SVX"}
        self.ready = {}

    def starts(self, step):
        kind, start = step[0], self.free["PE"]
        if kind == "v" and ("pv", QUADS - 1, KEY_TILES[-1], 1) not in self.ready:
            return None
        if kind == "st":
            before = TT * step[1] + place_of(step[2]) - 2
            if before >= 0 and ("pv", before // TT, KEY_TILES[before % TT], 1) not in self.ready:
                return None
        for other in needs(step):
            if other not in self.ready:
                return None
            start = max(start, self.ready[other] + LATENCY)
        if kind in RING and kind != "pv" and (kind not in ("gu", "dn") or step[3] == 0):
            start = max(start, self.slots[RING[kind]][0] + LATENCY)
        if kind in ("mt", "xt"):
            start = max(start, self.free["DVE"] + LATENCY)
        return start

    def emit(self, step):
        kind, now = step[0], self.starts(step)
        pe, others = work(step)
        if kind in RING:
            self.free["PE"] = now = now + pe
        for engine, time in others:
            self.free[engine] = now = max(self.free[engine], now + LATENCY) + time
            if kind == "dn" and engine == "ACT":
                free = now
        if kind in RING and kind != "pv" and ends(step):
            slots = self.slots[RING[kind]]
            slots.pop(0)
            slots.append(free if kind == "dn" else now)
        self.ready[step[:3] if kind in ("gu", "dn") else step] = now + DMA_TIME.get(kind, 0)

    def run(self, main, *sides):
        streams = [list(main)] + [list(side[0]) for side in sides]
        ranks = [0.0] + [side[1] for side in sides]
        spans = [None] + [side[1:] if len(side) == 3 else None for side in sides]
        total = [sum(map(weight, stream)) for stream in streams]
        done, result = [0.0] * len(streams), []
        while any(streams):
            best = None
            for i, stream in enumerate(streams):
                if not stream:
                    continue
                start = self.starts(stream[0])
                if start is None:
                    continue
                ahead = ranks[i]
                if spans[i]:
                    pace = (done[0] / total[0] - spans[i][0]) / (spans[i][1] - spans[i][0])
                    ahead = done[i] / total[i] - pace
                    if streams[0] and ahead > 0:
                        continue
                key = round(max(start - self.free["PE"], 0) / 50), ahead - (stream[0][0] == "st")
                if best is None or key < best[0]:
                    best = key, i
            i = best[1] if best else next(i for i, stream in enumerate(streams) if stream)
            step = streams[i].pop(0)
            done[i] += weight(step)
            self.emit(step)
            result.append(step)
        return result


def weight(step):
    pe, others = work(step)
    return pe + sum(time for _, time in others)


def place_of(kt):
    return KEY_TILES.index(kt)


def attention(quads):
    return ([("st", quad, kt, h) for quad in quads for kt in KEY_TILES for h in range(QUAD)],
            [("pv", quad, kt, half) for quad in quads for kt in KEY_TILES for half in range(kt // TC, 2)])


def project():
    return ([("xt", ch, c) for ch in range(NCH) for c in range(DT)]
            + [("q", dt, ch) for dt in range(DT) for ch in range(NCH)]
            + [("ckv", ch) for ch in range(NCH)]
            + [("k", dt, ch) for dt in range(DT) for ch in range(NCH)])


def values():
    return [("v", n) for n in range(TT // 2)]


def gates(ch):
    return [("gu", ch, jt, part) for jt in range(JT) for part in range(PARTS)]


def down(ch):
    steps = []
    for t in range(TC + 1):
        steps += [("dn", ch, t, part) for part in range(PARTS)] if t < TC else []
        steps += [("fin", ch, t - 1)] if t else []
    return steps


def after_attention():
    steps = []
    for t in range(TT + 2):
        for tag, tile in (("ct", t), ("cn", t - 1), ("wo", t - 2)):
            if 0 <= tile < TT:
                steps.append((tag, tile))
        if t - 2 in (TC - 1, TT - 1):
            steps += [("ln2", (t - 2) // TC, phase) for phase in range(3)]
    return steps


def schedule(segment):
    if segment not in schedules:
        schedules[segment] = make_schedule(segment)
    return schedules[segment]


schedules = {}


def make_schedule(segment):
    ahead = [step for quad in range(AHEAD) for step in maxima(1, quad)]
    if segment == "first":
        fold = ([("wug", c, n) for c in range(DT) for n in range(2 * J // CH)]
                + [("wd", n) for n in range(JT // 2)])
        return [("wq",), ("ln1",)] + project() + [("stack",)] + values() + [("mix",)] + fold + ahead
    more = segment == "body"
    merge = Merge()
    scores, products = attention(range(QUADS))
    sides = [([step for quad in range(AHEAD, QUADS) for step in maxima(0, quad)], 0.0, SA_END)]
    if more:
        sides.append(([("ln1",)] + project(), PROJECT_START, 0.97))
    steps = merge.run(scores, (products, 0.0), *sides)
    if more:
        steps.append(("stack",))
        merge.emit(("stack",))
    ffn = [("x2t", 0, c) for c in range(DT)] + gates(0) + [("x2t", 1, c) for c in range(DT)]
    ffn += gates(1)[:PARTS] + down(0) + gates(1)[PARTS:] + down(1)
    return steps + merge.run(ffn, (after_attention(), -0.5), (values() if more else [], 0.5),
                             (ahead if more else [], 0.0, 0.97))


RING = {"st": "S", "sa": "X", "mt": "X", "xt": "X", "q": "X", "ckv": "X", "v": "X", "k": "X",
        "ct": "S", "cn": "X", "wo": "V", "x2t": "X", "gu": "S", "dn": "V", "wq": "X", "wug": "S",
        "wd": "V"}


def ends(step):
    return step[0] not in ("gu", "dn") or step[3] == PARTS - 1


def results(segment):
    return [step[:3] if step[0] in ("gu", "dn") else step for step in schedule(segment) if ends(step)]


class PsumTurns:

    def __init__(self):
        self.place, self.count = {}, {}
        for segment in ("first", "body", "last"):
            turn, count = {"S": 0, "V": 0, "X": 0}, {}
            for step in schedule(segment):
                if step[0] == "pv":
                    slot, step = f"V{step[3]}", ("pv", step[1], step[3])
                    if (segment, step) in self.place:
                        continue
                elif step[0] in ("gu", "dn") and step[3]:
                    continue
                elif step[0] in RING:
                    ring = RING[step[0]]
                    slot = f"{ring}{turn[ring] % 2}"
                    turn[ring] += 1
                else:
                    continue
                if step[0] in ("gu", "dn"):
                    step = step[:3]
                self.place[segment, step] = slot, count.get(slot, 0)
                count[slot] = count.get(slot, 0) + 1
            self.count[segment] = count

    def of(self, segment, b, *step):
        slot, before = self.place[segment, step]
        if segment != "first":
            before = self.count["first"].get(slot, 0) + before + b * self.count["body"].get(slot, 0)
        return slot, before


LINKS = {"ln1": 1, "mix": 4, "mt": 2, "ct": 1, "wo": 1, "gu": 1, "dn": 1}


def links_of(step):
    return (0, 2, 0)[step[2]] if step[0] == "ln2" else LINKS.get(step[0], 0)


class Links:

    def __init__(self):
        self.total = {s: sum(links_of(step) for step in schedule(s) if ends(step))
                      for s in ("first", "body", "last")}
        self.now = 0

    def start(self, segment, b):
        assert segment == "first" or self.now == self.total[self.segment]
        self.segment, self.now = segment, 0
        self.base = 0 if segment == "first" else self.total["first"] + b * self.total["body"]

    def count(self):
        self.now += 1
        return self.base + self.now


def wait_past(engine, semaphore, count):
    if not (isinstance(count, int) and count == 0):
        engine.wait_ge(semaphore, count)


def layer(nc, x, w_dq, w_uq_t, w_dkv_t, w_uk_t, w_uv_t, w_o_t, b_o, su_ug, su_dp, wscale_ug,
          wscale_dp, w_up_t, w_gate_t, w_down_t, hadamard, identity, causal, out):
    turns = PsumTurns()
    links = Links()
    x_tiles = x.rearrange("b (t p) d -> b p t d", p=P)
    out_tiles = out.rearrange("b (t p) d -> b t p d", p=P)
    q_scratch = nc.dram_tensor("q_scratch", [3, H, DH, N], BF16, kind="Internal")
    k_scratch = nc.dram_tensor("k_scratch", [3, H, DH, N], BF16, kind="Internal")

    with ExitStack() as ctx:
        def sb(name, shape, dt=F32):
            return ctx.enter_context(nc.sbuf_tensor(name, shape, dt))

        def sem(name):
            return ctx.enter_context(nc.semaphore(name))

        psum = {}
        for ring, width in (("S", 2 * CH), ("V", CH), ("X", CH)):
            for i in range(2):
                psum[f"{ring}{i}"] = ctx.enter_context(nc.psum_tensor(f"psum_{ring}{i}", [P, width], F32))

        ident = sb("ident", [P, P])
        hada = sb("hada", [P, P])
        mask = sb("mask", [P, CH], BF16)
        wq = sb("wq", [P, DT, D])
        wdkv = sb("wdkv", [P, DT, P])
        wuk = sb("wuk", [P, D])
        wuv = sb("wuv", [P, D])
        wo = sb("wo", [P, DT, D])
        bo = sb("bo", [P, D])
        wug = sb("wug", [P, DT, 2 * J])
        wd = sb("wd", [P, JT, D])
        signs_ug = sb("signs_ug", [P, DT])
        signs_dp = sb("signs_dp", [P, JT])
        xa = sb("xa", [P, TT, D])
        xr = sb("xr", [P, TT, D])
        xT = sb("xT", [P, DT, N])
        ckvT = sb("ckvT", [P, N])
        parts = sb("parts", [P, 3, DT, N], BF16)
        rest = sb("rest", [P, 2, CH])
        q_stack = sb("q_stack", [P, H, N], BF16)
        k_stack = sb("k_stack", [P, H, N], BF16)
        v_ones = sb("v_ones", [P, TT, H * VW + 16])
        probs = sb("probs", [P, 2, QUAD, N])
        ctx_raw = sb("ctx_raw", [P, QUADS, N])
        ctx_n = sb("ctx_n", [P, 2, D])
        ctx_nT = sb("ctx_nT", [P, 2, D])
        row_max = sb("row_max", [P, QUAD, TT])
        row_max0 = sb("row_max0", [P, QUAD, TT - TC])
        max_rest = sb("max_rest", [QUAD * TT, P])
        max_parts = sb("max_parts", [QUAD * TT, 3, P], BF16)
        rden = sb("rden", [P, 2, H])
        norms = ("ln1", "lna", "lnx", "lnf")
        stats = {k: sb(f"stats_{k}", [P, TT, 6]) for k in norms}
        mv = {k: sb(f"mv_{k}", [P, TT, 2]) for k in norms}
        rstd = {k: sb(f"rstd_{k}", [P, TT]) for k in norms}
        var_eps = {k: sb(f"var_eps_{k}", [P, TT]) for k in norms}
        shift = {k: sb(f"shift_{k}", [P, TT]) for k in norms[1:]}
        scaled_mean = sb("scaled_mean", [P, TT])
        minus_half = sb("minus_half", [P, TT])
        zeros = sb("zeros", [P, TT])
        hT = [probs[:, i].rearrange("p h n -> p (h n)").rearrange("p (j n) -> p j n", j=JT) for i in range(2)]
        y = probs[:, 1, 0:2, :].rearrange("p a n -> p (a n)").rearrange("p (t d) -> p t d", d=D)
        spare = parts[:].rearrange("p s c n -> p (s c n)").bitcast(F32)
        tanh_g = spare[:, 0:2 * CH].rearrange("p (i n) -> p i n", i=2)
        gated = spare[:, 2 * CH:4 * CH].rearrange("p (i n) -> p i n", i=2)
        ffn_raw = spare[:, 4 * CH:5 * CH].rearrange("p (i n) -> p i n", i=2)
        ffn_n = spare[:, 5 * CH:6 * CH].rearrange("p (i n) -> p i n", i=2)
        w_raw = probs[:, 0].rearrange("p h n -> p (h n)").rearrange("p (c j) -> p c j", c=DT)
        w_mix = probs[:, 1].rearrange("p h n -> p (h n)").rearrange("p (c j) -> p c j", c=DT)
        d_mix = [ctx_raw[:, 2 * i:2 * i + 2, :].rearrange("p a n -> p (a n)") for i in range(2)]
        scale_ug = xr[:].rearrange("p t d -> p (t d)")
        scale_dp = ctx_nT[:, 0]
        w_dq_sb = q_stack[:, 0, :].bitcast(F32).rearrange("p (t c) -> p t c", t=DT)
        w_uq_sb = q_stack[:, 1, :].bitcast(F32).rearrange("p (t c) -> p t c", t=DT)

        psum_filled = {s: sem(f"psum_filled_{s}") for s in psum}
        psum_taken = {s: sem(f"psum_taken_{s}") for s in psum}
        proj_loaded = sem("proj_loaded")
        ffn_loaded = sem("ffn_loaded")
        xa_loaded = sem("xa_loaded")
        xr_loaded = sem("xr_loaded")
        out_stored = sem("out_stored")
        pads_ready = sem("pads_ready")
        w_mixed = sem("w_mixed")
        ln1_stats = sem("ln1_stats")
        root_steps = {k: sem(f"root_steps_{k}") for k in norms}
        xn_ready = sem("xn_ready")
        part0_ready = sem("part0_ready")
        part1_ready = sem("part1_ready")
        part2_ready = sem("part2_ready")
        parts_stored = sem("parts_stored")
        stacks_loaded = sem("stacks_loaded")
        row_max_ready = sem("row_max_ready")
        max_parts_ready = sem("max_parts_ready")
        max_loaded = sem("max_loaded")
        masked = sem("masked")
        ln2_stats = sem("ln2_stats")
        x2n_ready = sem("x2n_ready")
        tanh_ready = sem("tanh_ready")
        ln3_stats = sem("ln3_stats")
        ffn_ready = sem("ffn_ready")
        out_ready = sem("out_ready")
        dve_done = sem("dve_done")
        started = sem("started")

        block = ctx.enter_context(nc.Block())

        def segments(engine, emit):
            emit("first", -1)
            with engine.Fori(0, B - 1) as b:
                emit("body", b)
            emit("last", B - 1)

        def wait_apart(engine, semaphore, count):
            if not isinstance(count, int):
                engine.compute_val(count)
            engine.wait_ge(started, 1)
            engine.wait_ge(semaphore, count)

        def chunk(ch):
            return slice(CH * ch, CH * (ch + 1))

        @block.sync
        def _(sp):
            sp.dma_start(xa[:], x_tiles[0]).then_inc(xa_loaded, 16)
            sp.dma_start(w_dq_sb, w_dq.rearrange("(t p) c -> p t c", p=P)).then_inc(proj_loaded, 16)
            sp.dma_start(w_uq_sb, w_uq_t.rearrange("(t p) c -> p t c", p=P)).then_inc(proj_loaded, 16)
            sp.dma_start(ident[:], identity).then_inc(proj_loaded, 16)
            sp.wait_ge(pads_ready, 1)
            sp.dma_start(wdkv[:, :, 0:CKV], w_dkv_t.rearrange("(t p) c -> p t c", p=P)).then_inc(proj_loaded, 16)
            sp.dma_start(wuk[0:CKV, :], w_uk_t).then_inc(proj_loaded, 16)
            sp.dma_start(wuv[0:CKV, :], w_uv_t).then_inc(proj_loaded, 16)
            for dst, src in (
                (w_raw[:, :, 0:J], w_up_t.rearrange("(t p) j -> p t j", p=P)),
                (w_raw[:, :, J:2 * J], w_gate_t.rearrange("(t p) j -> p t j", p=P)),
                (d_mix[0].rearrange("p (t c) -> p t c", c=D), w_down_t.rearrange("(t p) c -> p t c", p=P)),
                (hada[:], hadamard), (mask[:], causal),
                (signs_ug[:], su_ug),
                (signs_dp[:], su_dp),
                (scale_ug, wscale_ug.partition_broadcast(P)), (scale_dp, wscale_dp.partition_broadcast(P)),
                (bo[:], b_o.partition_broadcast(P)), (wo[:], w_o_t.rearrange("(t p) c -> p t c", p=P)),
            ):
                sp.dma_start(dst, src).then_inc(ffn_loaded, 16)

            def store_parts(i, which):
                scratch = (q_scratch, k_scratch)[which]
                wait_apart(sp, part2_ready, 8 * i + 4 * which + 4)
                if not (isinstance(i, int) and i == 0):
                    wait_apart(sp, stacks_loaded, 16 * 12 * i)
                for s in range(3):
                    sp.dma_start(scratch[s].rearrange("(t h) p n -> (h p) t n", t=DT), parts[:, s])\
                      .then_inc(parts_stored, 16)

            def load_stacks(i):
                for which, stack, scratch in ((0, q_stack, q_scratch), (1, k_stack, k_scratch)):
                    sp.wait_ge(parts_stored, 48 * (2 * i + which + 1))
                    for s, pair in enumerate(STRIPS):
                        sp.dma_start(stack[DH * s:DH * (s + 1)], scratch[pair[which]].rearrange("h p n -> p h n"))\
                          .then_inc(stacks_loaded, 16)

            def emit(segment, b):
                for step in results(segment):
                    kind = step[0]
                    if kind in ("q", "k") and step[1:] == (DT - 1, NCH - 1):
                        store_parts(b + 1, 0 if kind == "q" else 1)
                    if kind == "stack":
                        if segment == "body":
                            slot, before = turns.of(segment, b, "st", QUADS - 1, KEY_TILES[-1], QUAD - 1)
                            wait_apart(sp, psum_filled[slot], before + 1)
                        load_stacks(b + 1)
                    if kind == "mt":
                        _, ahead, quad = step
                        sp.wait_ge(max_parts_ready, QUADS * (b + ahead) + quad + 1)
                        for j in range(3):
                            row = q_stack[KS + j:KS + j + 1, QUAD * quad:QUAD * (quad + 1), :]
                            sp.dma_start(row.rearrange("o h (t n) -> o (h t) n", n=P), max_parts[:, j, :])\
                              .then_inc(max_loaded, 16)
                    if step == ("st", 0, 0, 0) and segment == "body":
                        slot, before = turns.of(segment, b, *step)
                        wait_apart(sp, psum_filled[slot], before + 1)
                        sp.dma_start(xa[:], x_tiles[b + 1]).then_inc(xa_loaded, 16)
                    if kind == "fin":
                        t = TC * step[1] + step[2]
                        wait_apart(sp, out_ready, b * TT + t + 1)
                        sp.dma_start(out_tiles[b, t], xr[:, t, :]).then_inc(out_stored, 16)
                if segment == "first":
                    for n in (2 * J // CH - 2, 2 * J // CH - 1):
                        slot, before = turns.of(segment, b, "wug", DT - 1, n)
                        sp.wait_ge(psum_taken[slot], before + 1)
                    sp.dma_start(xr[:], x_tiles[0]).then_inc(xr_loaded, 16)
                if segment == "body":
                    wait_apart(sp, out_stored, 16 * TT * (b + 1))
                    sp.dma_start(xr[:], x_tiles[b + 1]).then_inc(xr_loaded, 16)

            segments(sp, emit)
            sp.wait_ge(out_stored, 16 * TT * B)

        @block.gpsimd
        def _(pool):
            nc.gpsimd.memset(minus_half[:], -0.5).then_inc(started, 1)
            nc.gpsimd.memset(zeros[:], 0.0)
            nc.gpsimd.memset(wdkv[:], 0.0)
            nc.gpsimd.memset(wuk[:], 0.0)
            nc.gpsimd.memset(wuv[:], 0.0).then_inc(pads_ready, 1)
            nc.gpsimd.memset(v_ones[:, :, H * VW:], 0.0)
            nc.gpsimd.memset(v_ones[:, :, 0:H * VW].rearrange("p t (h w) -> p t h w", w=VW)[:, :, :, DH:VW], 1.0)\
              .then_inc(pads_ready, 1)

            def root(key, rows, n):
                before = ROOT_STEPS[key] * (n - 1)
                nc.gpsimd.tensor_scalar(var_eps[key][:, rows], mv[key][:, rows, 1], EPS, None, ALU.add)\
                  .then_inc(root_steps[key], 1)
                pool.wait_ge(root_steps[key], before + 1)
                nc.gpsimd.tensor_tensor(rstd[key][:, rows], var_eps[key][:, rows], minus_half[:, rows], ALU.pow)\
                  .then_inc(root_steps[key], 1)
                if key == "ln1":
                    return
                pool.wait_ge(root_steps[key], before + 2)
                nc.gpsimd.tensor_tensor(scaled_mean[:, rows], mv[key][:, rows, 0], rstd[key][:, rows], ALU.mult)\
                  .then_inc(root_steps[key], 1)
                pool.wait_ge(root_steps[key], before + 3)
                nc.gpsimd.tensor_tensor(shift[key][:, rows], (shift["lna"] if key == "lnf" else zeros)[:, rows],
                                        scaled_mean[:, rows], ALU.subtract).then_inc(root_steps[key], 1)

            pool.wait_ge(pads_ready, 2)

            def emit(segment, b):
                splits = 0
                for step in results(segment):
                    kind = step[0]
                    if kind == "ln1":
                        wait_apart(pool, ln1_stats, b + 2)
                        root("ln1", slice(0, TT), b + 2)
                    if kind == "mix":
                        pool.wait_ge(part2_ready, 8)
                        nc.gpsimd.memset(k_stack[KS:P], 1.0).then_inc(pads_ready, 1)
                        pool.wait_ge(pads_ready, 3)
                    if kind in ("q", "k"):
                        _, dt, ch = step
                        pool.wait_ge(part1_ready, 8 * (b + 1) + splits + 1)
                        nc.gpsimd.tensor_tensor(parts[:, 2, dt, chunk(ch)], rest[:, splits % 2],
                                                parts[:, 1, dt, chunk(ch)], ALU.subtract).then_inc(part2_ready, 1)
                        splits += 1
                    if kind == "st":
                        _, quad, kt, h = step
                        slot, before = turns.of(segment, b, *step)
                        if h < QUAD - 2:
                            continue
                        wait_apart(pool, psum_taken[slot], before + 1)
                        if h < QUAD - 1:
                            continue
                        tile = probs[:, place_of(kt) % 2, :, kt * P:(kt + 1) * P]
                        nc.gpsimd.affine_select(out=tile, in_=tile, compare_op=ALU.is_ge, fill=0.0, base=0,
                                                pattern=[[0, QUAD], [1, P]], channel_multiplier=-1).then_inc(masked, 1)
                    if kind == "ln2" and step[2] < 2:
                        _, ch, phase = step
                        wait_apart(pool, ln2_stats, b * 2 * NCH + 2 * ch + phase + 1)
                        root(("lna", "lnx")[phase], slice(TC * ch, TC * (ch + 1)), b * NCH + ch + 1)
                    if kind == "dn":
                        t = TC * step[1] + step[2]
                        wait_apart(pool, ln3_stats, b * TT + t + 1)
                        root("lnf", slice(t, t + 1), b * TT + t + 1)
                    if kind == "fin":
                        t = TC * step[1] + step[2]
                        pool.wait_ge(ffn_ready, b * TT + t + 1)
                        nc.gpsimd.tensor_tensor(xr[:, t, :], xr[:, t, :], ffn_n[:, t % 2], ALU.add)\
                          .then_inc(out_ready, 1)

            segments(pool, emit)

        @block.scalar
        def _(act):
            def emit(segment, b):
                splits = 0
                for step in results(segment):
                    kind = step[0]
                    if kind in ("wq", "xt", "x2t", "q", "k", "ckv", "v", "st", "cn", "gu", "dn"):
                        slot, before = turns.of(segment, b, *step)
                        src = psum[slot]
                    if kind in ("q", "k") and splits % 4 == 0:
                        wait_past(act, parts_stored, 48 * (2 * (b + 1) + splits // 4))
                    if step == ("gu", 0, 0):
                        act.wait_ge(parts_stored, 48 * 2 * (b + 2 if segment == "body" else B))
                    if kind in ("wq", "xt", "x2t", "q", "k", "ckv", "v", "st", "cn", "gu", "dn"):
                        act.wait_ge(psum_filled[slot], before + 1)
                    if kind == "wq":
                        nc.scalar.activation(wq[:].rearrange("p c d -> p (c d)"), src[:], ACT.Copy)\
                          .then_inc(psum_taken[slot], 1)
                    if kind in ("xt", "x2t"):
                        _, ch, c = step
                        nc.scalar.activation(xT[:, c, chunk(ch)], src[:], ACT.Copy).then_inc(psum_taken[slot], 1)
                    if kind in ("q", "k"):
                        _, dt, ch = step
                        nc.scalar.activation(parts[:, 0, dt, chunk(ch)], src[:], ACT.Copy).then_inc(part0_ready, 1)
                        splits += 1
                    if kind == "ckv":
                        nc.scalar.activation(ckvT[:, chunk(step[1])], src[:], ACT.Copy).then_inc(psum_taken[slot], 1)
                    if kind == "v":
                        n = step[1]
                        dst = v_ones[:, 2 * n:2 * n + 2, 0:H * VW].rearrange("p t (h w) -> p t h w", w=VW)
                        nc.scalar.activation(dst[:, :, :, 0:DH], src[:].rearrange("p (t h w) -> p t h w", t=2, w=DH),
                                             ACT.Copy).then_inc(psum_taken[slot], 1)
                    if kind == "st":
                        _, quad, kt, h = step
                        nc.scalar.activation(probs[:, place_of(kt) % 2, h, kt * P:], src[:, kt * P:], ACT.Exp,
                                             scale=DH ** -0.5).then_inc(psum_taken[slot], 1)
                    if kind == "pv" and step[2] == LAST_KEYS[step[3]]:
                        _, quad, _, half = step
                        slot, before = turns.of(segment, b, "pv", quad, half)
                        act.wait_ge(psum_filled[slot], before + 1)
                        nc.scalar.activation(ctx_raw[:, quad, chunk(half)], psum[slot][:], ACT.Copy)\
                          .then_inc(psum_taken[slot], 1)
                    if kind == "cn":
                        nc.scalar.activation(ctx_nT[:, step[1] % 2], src[:, 0:D], ACT.Copy)\
                          .then_inc(psum_taken[slot], 1)
                    if kind == "gu":
                        nc.scalar.activation(tanh_g[:, step[2] % 2], src[:, 0:CH], ACT.Tanh, scale=0.5)\
                          .then_inc(tanh_ready, 1)
                    if kind == "ln2" and step[2] == 2:
                        ch = step[1]
                        act.wait_ge(root_steps["lnx"], ROOT_STEPS["lnx"] * (b * NCH + ch + 1))
                        for t in range(TC * ch, TC * (ch + 1)):
                            last = nc.scalar.activation(y[:, t, :], xr[:, t, :], ACT.Identity,
                                                        bias=shift["lnx"][:, t:t + 1], scale=rstd["lnx"][:, t:t + 1])
                        last.then_inc(x2n_ready, 1)
                    if kind == "dn":
                        t = TC * step[1] + step[2]
                        if t > 1:
                            act.wait_ge(ffn_ready, b * TT + t - 1)
                        nc.scalar.activation(ffn_raw[:, t % 2], src[:, 0:D], ACT.Copy).then_inc(psum_taken[slot], 1)
                    if kind == "fin":
                        t = TC * step[1] + step[2]
                        act.wait_ge(root_steps["lnf"], ROOT_STEPS["lnf"] * (b * TT + t + 1))
                        if t > 1:
                            act.wait_ge(out_ready, b * TT + t - 1)
                        nc.scalar.activation(ffn_n[:, t % 2], ffn_raw[:, t % 2], ACT.Identity,
                                             bias=shift["lnf"][:, t:t + 1], scale=rstd["lnf"][:, t:t + 1])\
                          .then_inc(ffn_ready, 1)

            segments(act, emit)

        @block.vector
        def _(dve):
            def moments(key, tile, source):
                return nc.vector.bn_stats(stats[key][:, tile, :], source)

            def aggregate(key, tile):
                return nc.vector.bn_aggr(mv[key][:, tile, :], stats[key][:, tile, :])

            def normalise(dst, source, key, t):
                return nc.vector.tensor_scalar(dst, source, mv[key][:, t, 0:1], rstd[key][:, t:t + 1],
                                               ALU.subtract, ALU.mult)

            def emit(segment, b):
                links.start(segment, b)
                splits = 0
                for step in results(segment):
                    kind = step[0]
                    if kind in ("sa", "mt", "q", "k", "ct", "wo", "gu", "dn", "wug", "wd"):
                        slot, before = turns.of(segment, b, *step)
                        src = psum[slot]
                        if kind == "sa":
                            wait_apart(dve, psum_filled[slot], before + 1)
                        elif kind not in ("mt", "q", "k", "dn"):
                            dve.wait_ge(psum_filled[slot], before + 1)
                    if kind == "sa":
                        _, _, quad, h, qt, k0, keys = step
                        if k0 + keys < (qt + 1) * P:
                            nc.vector.tensor_reduce(row_max0[:, h, qt - TC:qt - TC + 1], src[:, 0:keys], AX_X, ALU.max)\
                              .then_inc(psum_taken[slot], 1)
                        else:
                            nc.vector.tensor_tensor_reduce(src[:, 0:keys], src[:, 0:keys], mask[:, CH - keys:CH],
                                                           1.0, MASKED, ALU.add, ALU.max,
                                                           row_max[:, h, qt:qt + 1]).then_inc(psum_taken[slot], 1)
                            last_piece = slot, before
                    if kind == "mt":
                        _, ahead, quad = step
                        dve.wait_ge(psum_taken[last_piece[0]], last_piece[1] + 1)
                        nc.vector.tensor_tensor(row_max[:, :, TC:TT], row_max[:, :, TC:TT], row_max0[:], ALU.max)\
                          .then_inc(row_max_ready, 1)
                        dve.wait_ge(psum_filled[slot], before + 1)
                        wait_past(dve, max_loaded, 48 * (QUADS * (b + ahead) + quad))
                        done = links.count()
                        nc.vector.tensor_scalar(max_parts[:, 0, :], src[0:QUAD * TT, 0:P], -1.0, None, ALU.mult)\
                          .then_inc(dve_done, 1)
                        dve.wait_ge(dve_done, done)
                        done = links.count()
                        nc.vector.scalar_tensor_tensor(out=max_rest[:], in0=src[0:QUAD * TT, 0:P], scalar=-1.0,
                                                       in1=max_parts[:, 0, :], op0=ALU.mult, op1=ALU.subtract)\
                          .then_inc(psum_taken[slot], 1)
                        dve.wait_ge(psum_taken[slot], before + 1)
                        nc.vector.tensor_copy(max_parts[:, 1, :], max_rest[:]).then_inc(dve_done, 1)
                        dve.wait_ge(dve_done, done)
                        nc.vector.tensor_tensor(max_parts[:, 2, :], max_rest[:], max_parts[:, 1, :], ALU.subtract)\
                          .then_inc(max_parts_ready, 1)
                    if kind == "ln1":
                        dve.wait_ge(xa_loaded, 16 * (b + 2))
                        for t in range(TT):
                            last = moments("ln1", t, xa[:, t, :])
                        done = links.count()
                        last.then_inc(dve_done, 1)
                        wait_apart(dve, dve_done, done)
                        for t in range(TT):
                            last = aggregate("ln1", t)
                        last.then_inc(ln1_stats, 1)
                        dve.wait_ge(ln1_stats, b + 2)
                        dve.wait_ge(root_steps["ln1"], ROOT_STEPS["ln1"] * (b + 2))
                        for t in range(TT):
                            last = normalise(xa[:, t, :], xa[:, t, :], "ln1", t)
                        last.then_inc(xn_ready, 1)
                    if kind in ("q", "k"):
                        _, dt, ch = step
                        n = 8 * (b + 1) + splits
                        if splits > 1:
                            dve.wait_ge(part2_ready, n - 1)
                        dve.wait_ge(part0_ready, n + 1)
                        nc.vector.tensor_tensor(rest[:, splits % 2], src[:], parts[:, 0, dt, chunk(ch)], ALU.subtract)\
                          .then_inc(psum_taken[slot], 1)
                        dve.wait_ge(psum_taken[slot], before + 1)
                        nc.vector.tensor_copy(parts[:, 1, dt, chunk(ch)], rest[:, splits % 2])\
                          .then_inc(part1_ready, 1)
                        splits += 1
                    if kind == "ct":
                        t = step[1]
                        heads = src[:, 0:CH].rearrange("p (h w) -> p h w", h=H)
                        done = links.count()
                        nc.vector.reciprocal(rden[:, t % 2, :], heads[:, :, DH]).then_inc(dve_done, 1)
                        dve.wait_ge(dve_done, done)
                        if t > 1:
                            other, uses = turns.of(segment, b, "cn", t - 2)
                            dve.wait_ge(psum_filled[other], uses + 1)
                        nc.vector.tensor_tensor(ctx_n[:, t % 2].rearrange("p (h w) -> p h w", h=H), heads[:, :, 0:DH],
                                                rden[:, t % 2, :].unsqueeze(2).broadcast_to((P, H, DH)), ALU.mult)\
                          .then_inc(psum_taken[slot], 1)
                    if kind == "wo":
                        t = step[1]
                        nc.vector.tensor_tensor(y[:, t, :], src[:, 0:D], bo[:], ALU.add).then_inc(psum_taken[slot], 1)
                        dve.wait_ge(psum_taken[slot], before + 1)
                        done = links.count()
                        moments("lna", t, y[:, t, :]).then_inc(dve_done, 1)
                    if kind == "ln2" and step[2] == 0:
                        ch = step[1]
                        wait_apart(dve, dve_done, done)
                        for t in range(TC * ch, TC * (ch + 1)):
                            last = aggregate("lna", t)
                        last.then_inc(ln2_stats, 1)
                    if kind == "ln2" and step[2] == 1:
                        ch = step[1]
                        tiles = range(TC * ch, TC * (ch + 1))
                        dve.wait_ge(root_steps["lna"], ROOT_STEPS["lna"] * (b * NCH + ch) + 2)
                        dve.wait_ge(xr_loaded, 16 * (b + 1))
                        for t in tiles:
                            last = nc.vector.scalar_tensor_tensor(out=xr[:, t, :], in0=y[:, t, :],
                                                                  scalar=rstd["lna"][:, t:t + 1], in1=xr[:, t, :],
                                                                  op0=ALU.mult, op1=ALU.add)
                        done = links.count()
                        last.then_inc(dve_done, 1)
                        dve.wait_ge(dve_done, done)
                        for t in tiles:
                            last = moments("lnx", t, xr[:, t, :])
                        done = links.count()
                        last.then_inc(dve_done, 1)
                        wait_apart(dve, dve_done, done)
                        for t in tiles:
                            last = aggregate("lnx", t)
                        last.then_inc(ln2_stats, 1)
                    if kind == "gu":
                        _, ch, jt = step
                        dve.wait_ge(tanh_ready, b * NCH * JT + JT * ch + jt + 1)
                        done = links.count()
                        nc.vector.scalar_tensor_tensor(out=gated[:, jt % 2], in0=tanh_g[:, jt % 2], scalar=1.0,
                                                       in1=src[:, 0:CH], op0=ALU.add, op1=ALU.mult)\
                          .then_inc(dve_done, 1)
                        dve.wait_ge(dve_done, done)
                        nc.vector.tensor_tensor(hT[ch][:, jt, :], gated[:, jt % 2], src[:, CH:2 * CH], ALU.mult)\
                          .then_inc(psum_taken[slot], 1)
                    if kind == "dn":
                        t = TC * step[1] + step[2]
                        wait_apart(dve, psum_taken[slot], before + 1)
                        done = links.count()
                        moments("lnf", t, ffn_raw[:, t % 2]).then_inc(dve_done, 1)
                        wait_apart(dve, dve_done, done)
                        aggregate("lnf", t).then_inc(ln3_stats, 1)
                    if kind == "mix":
                        dve.wait_ge(ffn_loaded, 16 * 11)
                        nc.vector.tensor_tensor(w_mix[:, 0], w_raw[:, 0], w_raw[:, 1], ALU.add)
                        nc.vector.tensor_tensor(w_mix[:, 1], w_raw[:, 0], w_raw[:, 1], ALU.subtract)
                        nc.vector.tensor_scalar(signs_ug[:], signs_ug[:], D ** -0.5, None, ALU.mult)
                        done = links.count()
                        nc.vector.tensor_scalar(signs_dp[:], signs_dp[:], 0.5 * J ** -0.5, None, ALU.mult)\
                          .then_inc(dve_done, 1)
                        for stage in range(3):
                            a, z = (m.rearrange("p (o two s) -> p o two s", two=2, s=D << stage)
                                    for m in (d_mix[stage % 2], d_mix[1 - stage % 2]))
                            dve.wait_ge(dve_done, done)
                            nc.vector.tensor_tensor(z[:, :, 0], a[:, :, 0], a[:, :, 1], ALU.add)
                            last = nc.vector.tensor_tensor(z[:, :, 1], a[:, :, 0], a[:, :, 1], ALU.subtract)
                            done = links.count()
                            last.then_inc(dve_done, 1)
                        dve.wait_ge(dve_done, done)
                    if kind == "wug":
                        _, c, n = step
                        nc.vector.scalar_tensor_tensor(out=wug[:, c, chunk(n)], in0=src[:, 0:CH], scalar=signs_ug[:, c:c + 1],
                                                       in1=scale_ug[:, chunk(n)], op0=ALU.mult, op1=ALU.mult)\
                          .then_inc(psum_taken[slot], 1)
                    if kind == "wd":
                        for i in range(2):
                            jt = 2 * step[1] + i
                            last = nc.vector.scalar_tensor_tensor(
                                out=wd[:, jt, :], in0=src[:, D * i:D * (i + 1)], scalar=signs_dp[:, jt:jt + 1],
                                in1=scale_dp, op0=ALU.mult, op1=ALU.mult)
                        last.then_inc(psum_taken[slot], 1)

            dve.wait_ge(ffn_loaded, 16 * 11)
            segments(dve, emit)

        @block.tensor
        def _(pe):
            def emit(segment, b):
                for step in schedule(segment):
                    kind = step[0]
                    if kind in RING:
                        part = step[3] if kind in ("gu", "dn") else 0
                        step = step[:3] if kind in ("gu", "dn") else step
                        slot, before = turns.of(segment, b, *step)
                        dst = psum[slot]
                        if kind != "mt" and part == 0:
                            wait_past(pe, psum_taken[slot], before)
                    if kind == "wq":
                        pe.wait_ge(proj_loaded, 16 * 6)
                        for ct in range(DT):
                            for t in range(DT):
                                last = nc.tensor.matmul(dst[:, D * ct:D * (ct + 1)], w_dq_sb[:, t, P * ct:P * (ct + 1)],
                                                        w_uq_sb[:, t, :], start=(t == 0), stop=(t == DT - 1))
                        last.then_inc(psum_filled[slot], 1)
                    if kind == "xt":
                        _, ch, c = step
                        pe.wait_ge(xn_ready, b + 2)
                        for t in range(TC):
                            last = nc.tensor.transpose(dst[:, P * t:P * (t + 1)],
                                                       xa[:, TC * ch + t, P * c:P * (c + 1)], ident[:])
                        last.then_inc(psum_filled[slot], 1)
                    if kind in ("q", "ckv"):
                        dt, ch = (step[1], step[2]) if kind == "q" else (0, step[1])
                        wait_taken(segment, b, slot, *(("xt", ch, c) for c in range(DT)))
                        if (kind, dt, ch) == ("q", 0, 0) and segment == "first":
                            wait_taken(segment, b, slot, ("wq",))
                        for c in range(DT):
                            w = wq[:, c, P * dt:P * (dt + 1)] if kind == "q" else wdkv[:, c, :]
                            last = nc.tensor.matmul(dst[:], w, xT[:, c, chunk(ch)], start=(c == 0), stop=(c == DT - 1))
                        last.then_inc(psum_filled[slot], 1)
                    if kind == "v":
                        n = step[1]
                        wait_taken(segment, b, slot, ("ckv", 2 * n // TC))
                        for i in range(2):
                            t = 2 * n + i
                            last = nc.tensor.matmul(dst[:, D * i:D * (i + 1)], ckvT[:, P * t:P * (t + 1)], wuv[:],
                                                    start=True, stop=True)
                        last.then_inc(psum_filled[slot], 1)
                    if kind == "k":
                        _, dt, ch = step
                        wait_taken(segment, b, slot, ("ckv", ch))
                        nc.tensor.matmul(dst[:], wuk[:, P * dt:P * (dt + 1)], ckvT[:, chunk(ch)], start=True, stop=True)\
                          .then_inc(psum_filled[slot], 1)
                    if kind == "sa":
                        _, ahead, quad, h, qt, k0, keys = step
                        head = QUAD * quad + h
                        if (quad, h, qt, k0) == (0, 0, 0, 0):
                            pe.wait_ge(stacks_loaded, 16 * 12 * (b + ahead + 1))
                        nc.tensor.matmul(dst[:, 0:keys], q_stack[0:KS, head, P * qt:P * (qt + 1)],
                                         k_stack[0:KS, head, k0:k0 + keys], start=True, stop=True)\
                          .then_inc(psum_filled[slot], 1)
                    if kind == "mt":
                        _, ahead, quad = step
                        pe.wait_ge(row_max_ready, QUADS * (b + ahead) + quad + 1)
                        wait_past(pe, psum_taken[slot], before)
                        nc.tensor.transpose(dst[0:QUAD * TT, 0:P], row_max[:].rearrange("p h t -> p (h t)"), ident[:])\
                          .then_inc(psum_filled[slot], 1)
                    if kind == "st":
                        _, quad, kt, h = step
                        head = QUAD * quad + h
                        if (kt, h) == (0, 0):
                            pe.wait_ge(max_loaded, 48 * (QUADS * b + quad + 1))
                        for q0 in range(kt * P // CH * CH, N, CH):
                            cols = slice(max(q0, kt * P), q0 + CH)
                            last = nc.tensor.matmul(dst[:, cols], k_stack[0:KM, head, P * kt:P * (kt + 1)],
                                                    q_stack[0:KM, head, cols], start=True, stop=True)
                        last.then_inc(psum_filled[slot], 1)
                    if kind == "pv":
                        _, quad, kt, half = step
                        slot, before = turns.of(segment, b, "pv", quad, half)
                        if kt == 0:
                            wait_past(pe, psum_taken[slot], before)
                        pe.wait_ge(masked, (b * QUADS + quad) * TT + place_of(kt) + 1)
                        q0 = max(CH * half, kt * P)
                        last_keys = kt == LAST_KEYS[half]
                        for h in range(QUAD):
                            col = VW * (QUAD * quad + h)
                            last = nc.tensor.matmul(psum[slot][32 * h:32 * (h + 1), q0 - CH * half:CH],
                                                    v_ones[:, kt, col:col + 32], probs[:, place_of(kt) % 2, h, q0:CH * (half + 1)],
                                                    start=(kt == 0), stop=last_keys, skip_group_check=True)
                        if last_keys:
                            last.then_inc(psum_filled[slot], 1)
                    if kind == "ct":
                        t = step[1]
                        if t == 0:
                            wait_taken(segment, b, slot, *(("pv", QUADS - 1, half) for half in range(2)))
                        for quad in range(QUADS):
                            last = nc.tensor.transpose(dst[:, P * quad:P * (quad + 1)],
                                                       ctx_raw[:, quad, P * t:P * (t + 1)], ident[:])
                        last.then_inc(psum_filled[slot], 1)
                    if kind == "cn":
                        t = step[1]
                        wait_taken(segment, b, slot, ("ct", t))
                        for c in range(DT):
                            last = nc.tensor.transpose(dst[:, P * c:P * (c + 1)], ctx_n[:, t % 2, P * c:P * (c + 1)],
                                                       ident[:])
                        last.then_inc(psum_filled[slot], 1)
                    if kind == "wo":
                        t = step[1]
                        wait_taken(segment, b, slot, ("cn", t))
                        for c in range(DT):
                            last = nc.tensor.matmul(dst[:, 0:D], ctx_nT[:, t % 2, P * c:P * (c + 1)], wo[:, c, :],
                                                    start=(c == 0), stop=(c == DT - 1))
                        last.then_inc(psum_filled[slot], 1)
                    if kind == "x2t":
                        _, ch, c = step
                        pe.wait_ge(x2n_ready, b * NCH + ch + 1)
                        for t in range(TC):
                            last = nc.tensor.transpose(dst[:, P * t:P * (t + 1)], y[:, TC * ch + t, P * c:P * (c + 1)],
                                                       ident[:])
                        last.then_inc(psum_filled[slot], 1)
                    if kind == "gu":
                        _, ch, jt = step
                        if part == 0:
                            wait_taken(segment, b, slot, *(("x2t", ch, c) for c in range(DT)))
                        i, c = divmod(part, DT)
                        j0 = (J, 0)[i] + P * jt
                        last = nc.tensor.matmul(dst[:, CH * i:CH * (i + 1)], wug[:, c, j0:j0 + P], xT[:, c, chunk(ch)],
                                                start=(c == 0), stop=(c == DT - 1))
                        if part == PARTS - 1:
                            last.then_inc(psum_filled[slot], 1)
                    if kind == "dn":
                        _, ch, t = step
                        if part == 0:
                            wait_taken(segment, b, slot, ("gu", ch, JT - 1))
                        for jt in range(JT // PARTS * part, JT // PARTS * (part + 1)):
                            last = nc.tensor.matmul(dst[:, 0:D], hT[ch][:, jt, P * t:P * (t + 1)], wd[:, jt, :],
                                                    start=(jt == 0), stop=(jt == JT - 1))
                        if part == PARTS - 1:
                            last.then_inc(psum_filled[slot], 1)
                    if kind in ("wug", "wd"):
                        if step == ("wug", 0, 0):
                            pe.wait_ge(dve_done, LINKS["ln1"] + LINKS["mix"])
                            pe.wait_ge(ffn_loaded, 16 * 11)
                        rhs = w_mix[:, step[1], chunk(step[2])] if kind == "wug" else d_mix[1][:, chunk(step[1])]
                        nc.tensor.matmul(dst[:, 0:CH], hada[:], rhs, start=True, stop=True).then_inc(psum_filled[slot], 1)
                if segment == "first":
                    wait_taken(segment, b, None, ("wd", JT // 2 - 1))
                    pe.wait_ge(pads_ready, 3)

            def wait_taken(segment, b, own, *steps):
                places = dict(turns.of(segment, b, *step) for step in steps)
                for slot, before in places.items():
                    if slot != own:
                        pe.wait_ge(psum_taken[slot], before + 1)

            segments(pe, emit)



def kernel(**inputs):
    import numpy as np
    import concourse.bacc as bacc
    from concourse.bass_utils import run_bass_kernel_spmd

    a = {k[3:]: np.asarray(v) for k, v in inputs.items()}
    sylvester = np.ones((1, 1), np.float32)
    while len(sylvester) < P:
        sylvester = np.block([[sylvester, sylvester], [sylvester, -sylvester]])
    bf16 = mybir.dt.np(BF16)
    causal = np.zeros((P, CH), np.float32)
    causal[:, CH - P:] = np.where(np.arange(P)[None, :] > np.arange(P)[:, None], MASKED, 0.0)
    arrays = {
        "x": a["attn_x"], "w_dq": a["attn_W_DQ"], "w_uq_t": a["attn_W_UQ"].T, "w_dkv_t": a["attn_W_DKV"].T,
        "w_uk_t": a["attn_W_UK"].T, "w_uv_t": a["attn_W_UV"].T, "w_o_t": a["attn_W_O"].T, "b_o": a["attn_b_O"],
        "su_ug": a["ffn_SU_ug"].reshape(DT, P).T, "su_dp": a["ffn_SU_dp"].reshape(JT, P).T, "wscale_ug": a["ffn_Wscale_ug"],
        "wscale_dp": a["ffn_Wscale_dp"], "w_up_t": a["ffn_W_up"].T, "w_gate_t": a["ffn_W_gate"].T,
        "w_down_t": a["ffn_W_down"].T, "hadamard": sylvester, "identity": np.eye(P, dtype=np.float32),
        "causal": causal.astype(bf16),
    }
    arrays = {k: np.ascontiguousarray(v) for k, v in arrays.items()}
    nc = bacc.Bacc("TRN2", target_bir_lowering=False, num_devices=1)
    args = [nc.dram_tensor(k, v.shape, mybir.dt.from_np(v.dtype), kind="ExternalInput").ap()
            for k, v in arrays.items()]
    args.append(nc.dram_tensor("out", (B, N, D), F32, kind="ExternalOutput").ap())
    layer(nc, *args)
    result = run_bass_kernel_spmd(nc, [arrays], core_ids=[0])
    return result.results[0]["out"]
```

```python
from contextlib import ExitStack

import concourse.bass as bass
from concourse import mybir

P = 128
B, N, D = 4, 1024, 256
H, DH = 16, 16
CKV = 64
J = 1024
TT = N // P
CH = 512
NCH = N // CH
TC = CH // P
DT = D // P
JT = J // P
QUAD = 4
QUADS = H // QUAD
VW = DH + 1
FOLDS = (DT * 2 * J // CH, JT // 2)
STRIPS = [(0, 0), (0, 1), (0, 2), (1, 0), (1, 1), (2, 0)]
KS = len(STRIPS) * DH
STACK_LOADS = 2 * len(STRIPS)
KM = KS + 3
PACES = {"maxima": (-0.108, 0.612), "project": (0.547, 1.006), "maxima ahead": (-0.041, 0.817)}
RANKS = {"scores": -0.5, "after, early": -0.3, "after": -1, "values": 0.1, "down": -0.03}
SAME_TIME = 150
ROOT_STEPS = {"ln1": 2, "lna": 4, "lnx": 4, "lnf": 4}
AHEAD = 100
PARTS = 4
GATE_PART = DT - 1
KEY_TILES = [0, 1, 2, 3, 7, 6, 5, 4]
LAST_KEYS = (3, 4)
EPS = 1e-5
MASKED = -3.0e38

F32 = mybir.dt.float32
BF16 = mybir.dt.bfloat16
ALU = mybir.AluOpType
ACT = mybir.ActivationFunctionType
AX_X = mybir.AxisListType.X



def score_pieces():
    return [(h, qt, k0, min((qt + 1) * P - k0, CH))
            for h in range(QUAD) for qt in range(TT) for k0 in range(0, (qt + 1) * P, CH)]


def maxima(ahead, quad, rings="X"):
    return [("sa", ahead, quad) + piece + (rings[n % len(rings)],)
            for n, piece in enumerate(score_pieces())] + [("mt", ahead, quad)]


def all_maxima(ahead, rings="X"):
    return [step for quad in range(QUADS) for step in maxima(ahead, quad, rings)]


def ring_of(step):
    return step[7] if step[0] == "sa" else RING[step[0]]


def work(step):
    kind = step[0]
    if kind == "sa":
        return 0.42 * step[6], [("DVE", 70 + 1.04 * step[6])]
    if kind == "st":
        keys = (TT - step[2]) * P
        mask = [("Pool", 600)] if step[3] == QUAD - 1 else []
        return 0.42 * keys, [("ACT", 60 + 0.84 * keys)] + mask
    if kind == "pv":
        copy = [("ACT", 480)] if step[2] == LAST_KEYS[step[3]] else []
        return 1.83 * (CH * (step[3] + 1) - max(CH * step[3], step[2] * P)), copy
    if kind in ("gu", "dn") and not ends(step):
        return 860, [("ACT", 480)] if kind == "gu" and step[3] == GATE_PART else []
    if kind == "ln2":
        return 0, ([("DVE", 400), ("Pool", 1900)], [("DVE", 3200), ("Pool", 1900)], [("ACT", 1800)])[step[2]]
    return {
        "wq": (3400, [("ACT", 480)]),
        "mix": (0, [("DVE", 5500)]),
        "wug": (860, [("ACT", 520), ("Pool", 1150)]),
        "wd": (860, [("ACT", 640), ("Pool", 1250)]),
        "ln1": (0, [("DVE", 3400), ("Pool", 1900), ("DVE", 2600)]),
        "xt": (860, [("ACT", 480)]),
        "q": (1720, [("ACT", 480), ("DVE", 700), ("DVE", 340), ("Pool", 1150)]),
        "ckv": (1720, [("ACT", 480)]),
        "k": (860, [("ACT", 480), ("DVE", 700), ("DVE", 340), ("Pool", 1150)]),
        "v": (860, [("ACT", 480)]),
        "stack": (0, []),
        "mt": (200, [("DVE", 1500)]),
        "ct": (430, [("DVE", 650)]),
        "cn": (215, [("ACT", 270)]),
        "wo": (860, [("DVE", 700)]),
        "x2t": (860, [("ACT", 480)]),
        "gu": (860, [("DVE", 1300)]),
        "dn": (860, [("ACT", 270), ("DVE", 550), ("Pool", 1500)]),
        "fin": (0, [("ACT", 450), ("Pool", 650)]),
    }[kind]


FREES_SLOT = {"dn": 0, "q": 1, "k": 1}


def needs(step):
    kind = step[0]
    if kind == "st" and step[2:] == (KEY_TILES[0], 0) and ("mt", 0, step[1]) in all_maxima(0)[AHEAD:]:
        return [("mt", 0, step[1])]
    if kind == "pv":
        return [("st", step[1], step[2], QUAD - 1)]
    if kind == "sa" and step[1]:
        return ["stacks"]
    if kind in ("q", "ckv"):
        return [("xt", step[-1], c) for c in range(DT)]
    if kind == "v":
        return [("ckv", 2 * step[1] // TC)]
    if kind == "k":
        return [("ckv", step[-1]), "q stored"]
    if kind == "stack":
        return [("k", DT - 1, NCH - 1), ("st", QUADS - 1, KEY_TILES[-1], QUAD - 1)]
    if kind == "ln2":
        return [("wo", TC * step[1] + TC - 1) if step[2] == 0 else ("ln2", step[1], step[2] - 1)]
    if step[:2] == ("dn", 1):
        return [("gu", 1, JT - 1), ("fin", 0, TC - 1)]
    if kind == "ct":
        half = step[1] // TC
        return [("pv", QUADS - 1, LAST_KEYS[half], half)]
    if kind == "gu":
        return [("x2t", step[1], c) for c in range(DT)]
    if kind == "x2t":
        return [("ln2", step[1], 2)]
    if kind == "dn":
        return [("gu", step[1], JT - 1)]
    return {"xt": [("ln1",)], "wug": [("mix", 0)], "wd": [("mix", 1)], "cn": [("ct", step[-1])],
            "wo": [("cn", step[-1])], "fin": [("dn",) + step[1:]]}.get(kind, [])


LATENCY = 190
DMA_TIME = {"mt": 4000, "q": 6500, "k": 15000}


class Merge:

    def __init__(self):
        self.free = {"PE": 0, "ACT": 0, "DVE": 0, "Pool": 0}
        self.slots = {ring: [0, 0] for ring in "SVX"}
        self.ready, self.more_needs = {}, {}
        self.thirds = [0, 0]

    def starts(self, step):
        kind, start = step[0], self.free["PE"]
        if kind == "v" and ("pv", QUADS - 1, KEY_TILES[-1], 1) not in self.ready:
            return None
        if kind == "st":
            before = read_before(step[1], step[2])
            if before and ("pv",) + before + (1,) not in self.ready:
                return None
        for other in needs(step) + self.more_needs.get(kind, []) + self.more_needs.get(step, []):
            if other not in self.ready:
                return None
            start = max(start, self.ready[other] + LATENCY)
        if kind in RING and (kind not in ("gu", "dn") or step[3] == 0):
            start = max(start, self.slots[ring_of(step)][0] + LATENCY)
        if kind in ("mt", "xt"):
            start = max(start, self.free["DVE"] + LATENCY)
        return start

    def emit(self, step):
        kind, now = step[0], self.starts(step)
        pe, others = work(step)
        if kind in RING or kind == "pv":
            self.free["PE"] = now = now + pe
        ends_at = []
        for n, (engine, time) in enumerate(others):
            now = max(self.free[engine], now + LATENCY)
            if kind in ("q", "k") and n == FREES_SLOT[kind]:
                now = max(now, self.thirds[0] + LATENCY)
            self.free[engine] = now = now + time
            ends_at.append(now)
        if kind in RING and ends(step):
            slots = self.slots[ring_of(step)]
            slots.pop(0)
            slots.append(ends_at[FREES_SLOT.get(kind, -1)])
        if kind in ("q", "k"):
            self.thirds = [self.thirds[1], now]
        if ends(step):
            self.ready[step[:3] if kind in ("gu", "dn") else step] = now + DMA_TIME["mt"] * (kind == "mt")
        if kind in ("q", "k") and step[1:] == (DT - 1, NCH - 1):
            self.ready["q stored" if kind == "q" else "stacks"] = now + DMA_TIME[kind]

    def run(self, main, *sides, carry=None):
        streams = [list(main)] + [list(side[0]) for side in sides] + [carry or []]
        ranks = [0.0] + [side[1] for side in sides] + [RANKS["after, early"]]
        spans = [None] + [side[1:] if len(side) == 3 else None for side in sides] + [None]
        total = [sum(map(weight, stream)) for stream in streams]
        done, result = [0.0] * len(streams), []
        while any(streams[:-1]):
            best = None
            for i, stream in enumerate(streams):
                if not stream:
                    continue
                start = self.starts(stream[0])
                if start is None:
                    continue
                ahead = ranks[i]
                if spans[i]:
                    pace = (done[0] / total[0] - spans[i][0]) / (spans[i][1] - spans[i][0])
                    ahead = done[i] / total[i] - pace
                    if streams[0] and ahead > 0:
                        continue
                if stream[0][0] == "st":
                    ahead += RANKS["scores"]
                key = round(max(start - self.free["PE"], 0) / SAME_TIME), ahead
                if best is None or key < best[0]:
                    best = key, i
            i = best[1] if best else next(i for i, stream in enumerate(streams) if stream)
            step = streams[i].pop(0)
            done[i] += weight(step)
            self.emit(step)
            result.append(step)
        return result


def weight(step):
    pe, others = work(step)
    return pe + sum(time for _, time in others)


def place_of(kt):
    return KEY_TILES.index(kt)


def probs_half(kt):
    return place_of(kt) % 2


def probs_column(kt, query):
    return query if kt <= TC else query - kt * P


def read_before(quad, kt):
    def columns(k):
        return set(range(probs_column(k, k * P), probs_column(k, N - 1) + 1, P))
    for n in range(TT * quad + place_of(kt) - 1, -1, -1):
        other = n // TT, KEY_TILES[n % TT]
        if probs_half(other[1]) == probs_half(kt) and columns(other[1]) & columns(kt):
            return other
    return None


def attention(quads):
    return ([("st", quad, kt, h) for quad in quads for kt in KEY_TILES for h in range(QUAD)],
            [("pv", quad, kt, half) for quad in quads for kt in KEY_TILES for half in range(kt // TC, 2)])


def project():
    return ([("xt", ch, c) for ch in range(NCH) for c in range(DT)]
            + [("q", dt, ch) for dt in range(DT) for ch in range(NCH)]
            + [("ckv", ch) for ch in range(NCH)]
            + [("k", dt, ch) for dt in range(DT) for ch in range(NCH)])


def values():
    return [("v", n) for n in range(TT // 2)]


def gates(ch):
    return [("gu", ch, jt, part) for jt in range(JT) for part in range(PARTS)]


def down(ch):
    steps = []
    for t in range(TC + 1):
        steps += [("dn", ch, t, part) for part in range(PARTS)] if t < TC else []
        steps += [("fin", ch, t - 1)] if t else []
    return steps


def after_attention():
    steps = []
    for t in range(TT + 2):
        for tag, tile in (("ct", t), ("cn", t - 1), ("wo", t - 2)):
            if 0 <= tile < TT:
                steps.append((tag, tile))
        if t - 2 in (TC - 1, TT - 1):
            steps += [("ln2", (t - 2) // TC, phase) for phase in range(3)]
    return steps


schedules = {}


def schedule(segment):
    if segment not in schedules:
        schedules[segment] = make_schedule(segment)
    return schedules[segment]


def make_schedule(segment):
    merge = Merge()
    if segment == "first":
        merge.ready.update({("pv", QUADS - 1, KEY_TILES[-1], 1): 0, ("st", QUADS - 1, KEY_TILES[-1], QUAD - 1): 0})
        steps = [("wq",), ("ln1",)] + project()
        at = steps.index(("k", 0, 0))
        steps = steps[:at] + [("mix", 0)] + steps[at:] + [("stack",), ("mix", 1)] + values()
        for step in steps:
            merge.emit(step)
        fold = ([("wug", c, n) for c in range(DT) for n in range(2 * J // CH)]
                + [("wd", n) for n in range(JT // 2)])
        return steps + merge.run(fold, (all_maxima(1, "XSV")[:AHEAD], -0.5))
    more = segment == "body"
    merge.free.update(ACT=3000, DVE=1500)
    scores, products = attention(range(QUADS))
    sides = [(all_maxima(0)[AHEAD:], *PACES["maxima"])]
    if more:
        sides.append(([("ln1",)] + project(), *PACES["project"]))
    after = after_attention()
    if more:
        merge.more_needs["q", DT - 1, NCH - 1] = [("mt", 0, QUADS - 1)]
        merge.more_needs["wo"] = [("xt", NCH - 1, DT - 1)]
    steps = merge.run(scores, (products, 0.0), *sides, carry=after)
    if more:
        steps.append(("stack",))
        merge.emit(("stack",))
    ffn = [("x2t", 0, c) for c in range(DT)] + gates(0) + [("x2t", 1, c) for c in range(DT)]
    ffn += gates(1) + down(1)
    return steps + merge.run(ffn, (down(0), RANKS["down"]), (after, RANKS["after"]),
                             (values() if more else [], RANKS["values"]),
                             (all_maxima(1)[:AHEAD] if more else [], *PACES["maxima ahead"]))


RING = {"st": "S", "sa": "X", "mt": "X", "xt": "X", "q": "X", "ckv": "X", "v": "X", "k": "X",
        "ct": "S", "cn": "X", "wo": "X", "x2t": "X", "gu": "S", "dn": "V", "wq": "X", "wug": "S",
        "wd": "V"}


def ends(step):
    return step[0] not in ("gu", "dn") or step[3] == PARTS - 1


def results(segment):
    gate = [("gate",) + step[1:3] if step[0] == "gu" and step[3] == GATE_PART else step
            for step in schedule(segment)]
    return [step[:3] if step[0] in ("gu", "dn") else step for step in gate if ends(step)]


class PsumTurns:

    def __init__(self):
        self.place, self.count = {}, {}
        for segment in ("first", "body", "last"):
            turn, count = {"S": 0, "V": 0, "X": 0}, {}
            for step in schedule(segment):
                if step[0] == "pv":
                    slot, step = f"V{step[3]}", ("pv", step[1], step[3])
                    if (segment, step) in self.place:
                        continue
                elif step[0] in ("gu", "dn") and step[3]:
                    continue
                elif step[0] in RING:
                    ring = ring_of(step)
                    slot = f"{ring}{turn[ring] % 2}"
                    turn[ring] += 1
                else:
                    continue
                if step[0] in ("gu", "dn"):
                    step = step[:3]
                self.place[segment, step] = slot, count.get(slot, 0)
                count[slot] = count.get(slot, 0) + 1
            self.count[segment] = count

    def of(self, segment, b, *step):
        slot, before = self.place[segment, step]
        if segment != "first":
            before = self.count["first"].get(slot, 0) + before + b * self.count["body"].get(slot, 0)
        return slot, before


LINKS = {"ln1": 1, "mt": 2, "ct": 1, "wo": 1, "gu": 1, "dn": 1}


def links_of(step):
    return (0, 2, 0)[step[2]] if step[0] == "ln2" else LINKS.get(step[0], 0)


class Links:

    def __init__(self):
        self.total = {s: sum(links_of(step) for step in schedule(s) if ends(step))
                      for s in ("first", "body", "last")}
        self.now = 0

    def start(self, segment, b):
        assert segment == "first" or self.now == self.total[self.segment]
        self.segment, self.now = segment, 0
        self.base = 0 if segment == "first" else self.total["first"] + b * self.total["body"]

    def count(self):
        self.now += 1
        return self.base + self.now


def wait_past(engine, semaphore, count):
    if not (isinstance(count, int) and count == 0):
        engine.wait_ge(semaphore, count)


def layer(nc, x, w_dq, w_uq_t, w_dkv_t, w_uk_t, w_uv_t, w_o_t, b_o, su_ug, su_dp, wscale_ug,
          wscale_dp, w_up_t, w_gate_t, w_down_t, hadamard, identity, causal, ones, out):
    turns = PsumTurns()
    links = Links()
    x_tiles = x.rearrange("b (t p) d -> b p t d", p=P)
    out_tiles = out.rearrange("b (t p) d -> b t p d", p=P)
    q_scratch = nc.dram_tensor("q_scratch", [3, H, DH, N], BF16, kind="Internal")
    k_scratch = nc.dram_tensor("k_scratch", [3, H, DH, N], BF16, kind="Internal")

    with ExitStack() as ctx:
        def sb(name, shape, dt=F32):
            return ctx.enter_context(nc.sbuf_tensor(name, shape, dt))

        def sem(name):
            return ctx.enter_context(nc.semaphore(name))

        psum = {}
        for ring, width in (("S", 2 * CH), ("V", CH), ("X", CH)):
            for i in range(2):
                psum[f"{ring}{i}"] = ctx.enter_context(nc.psum_tensor(f"psum_{ring}{i}", [P, width], F32))

        ident = sb("ident", [P, P])
        hada = sb("hada", [P, P])
        mask = sb("mask", [P, CH], BF16)
        wq = sb("wq", [P, DT, D])
        wdkv = sb("wdkv", [P, DT, P])
        wuk = sb("wuk", [P, D])
        wuv = sb("wuv", [P, D])
        wo = sb("wo", [P, DT, D])
        bo = sb("bo", [P, D])
        wug = sb("wug", [P, DT, 2 * J])
        wd = sb("wd", [P, JT, D])
        signs_ug = sb("signs_ug", [P, DT])
        signs_dp = sb("signs_dp", [P, JT])
        xa = sb("xa", [P, TT, D])
        xr = sb("xr", [P, TT, D])
        xT = sb("xT", [P, DT, N])
        ckvT = sb("ckvT", [P, N])
        parts = sb("parts", [P, 3, DT, N], BF16)
        rest = sb("rest", [P, 2, CH])
        q_stack = sb("q_stack", [P, H, N], BF16)
        k_stack = sb("k_stack", [P, H, N], BF16)
        v_ones = sb("v_ones", [P, TT, H * VW + 16])
        probs = sb("probs", [P, 2, QUAD, N])
        ctx_raw = sb("ctx_raw", [P, QUADS, N])
        ctx_n = sb("ctx_n", [P, 2, D])
        ctx_nT = sb("ctx_nT", [P, 2, D])
        row_max = sb("row_max", [P, QUAD, TT])
        row_max0 = sb("row_max0", [P, QUAD, TT - TC])
        max_rest = sb("max_rest", [QUAD * TT, P])
        max_parts = sb("max_parts", [QUAD * TT, 3, P], BF16)
        rden = sb("rden", [P, 2, H])
        norms = ("ln1", "lna", "lnx", "lnf")
        stats = {k: sb(f"stats_{k}", [P, TT, 6]) for k in norms}
        mv = {k: sb(f"mv_{k}", [P, TT, 2]) for k in norms}
        rstd = {k: sb(f"rstd_{k}", [P, TT]) for k in norms}
        var_eps = {k: sb(f"var_eps_{k}", [P, TT]) for k in norms}
        shift = {k: sb(f"shift_{k}", [P, TT]) for k in norms[1:]}
        scaled_mean = sb("scaled_mean", [P, TT])
        minus_half = sb("minus_half", [P, TT])
        zeros = sb("zeros", [P, TT])
        hT = [probs[:, i].rearrange("p h n -> p (h n)").rearrange("p (j n) -> p j n", j=JT) for i in range(2)]
        y = xa
        spare = parts[:].rearrange("p s c n -> p (s c n)").bitcast(F32)
        tanh_g = spare[:, 0:2 * CH].rearrange("p (i n) -> p i n", i=2)
        gated = spare[:, 2 * CH:4 * CH].rearrange("p (i n) -> p i n", i=2)
        ffn_raw = spare[:, 4 * CH:5 * CH].rearrange("p (i n) -> p i n", i=2)
        ffn_n = spare[:, 5 * CH:6 * CH].rearrange("p (i n) -> p i n", i=2)
        w_raw = probs[:, 0].rearrange("p h n -> p (h n)").rearrange("p (c j) -> p c j", c=DT)
        w_mix = probs[:, 1].rearrange("p h n -> p (h n)").rearrange("p (c j) -> p c j", c=DT)
        d_mix = [ctx_raw[:, 2 * i:2 * i + 2, :].rearrange("p a n -> p (a n)") for i in range(2)]
        scale_ug = xr[:].rearrange("p t d -> p (t d)")
        scale_dp = ctx_nT[:, 0]
        w_dq_sb = q_stack[:, 0, :].bitcast(F32).rearrange("p (t c) -> p t c", t=DT)
        w_uq_sb = q_stack[:, 1, :].bitcast(F32).rearrange("p (t c) -> p t c", t=DT)

        psum_filled = {s: sem(f"psum_filled_{s}") for s in psum}
        psum_taken = {s: sem(f"psum_taken_{s}") for s in psum}
        proj_loaded = sem("proj_loaded")
        ffn_loaded = sem("ffn_loaded")
        xa_loaded = sem("xa_loaded")
        xr_loaded = sem("xr_loaded")
        out_stored = sem("out_stored")
        pads_ready = sem("pads_ready")
        ones_loaded = sem("ones_loaded")
        w_mixed = sem("w_mixed")
        folded = sem("folded")
        ln1_stats = sem("ln1_stats")
        root_steps = {k: sem(f"root_steps_{k}") for k in norms}
        xn_ready = sem("xn_ready")
        part0_ready = sem("part0_ready")
        part1_ready = sem("part1_ready")
        part2_ready = sem("part2_ready")
        parts_stored = sem("parts_stored")
        early_loaded = sem("early_loaded")
        late_loaded = sem("late_loaded")
        row_max_ready = sem("row_max_ready")
        max_parts_ready = sem("max_parts_ready")
        max_loaded = sem("max_loaded")
        masked = sem("masked")
        ln2_stats = sem("ln2_stats")
        x2n_ready = sem("x2n_ready")
        gate_filled = sem("gate_filled")
        tanh_ready = sem("tanh_ready")
        ln3_stats = sem("ln3_stats")
        ffn_ready = sem("ffn_ready")
        out_ready = sem("out_ready")
        dve_done = sem("dve_done")
        started = sem("started")

        block = ctx.enter_context(nc.Block())

        def segments(engine, emit):
            emit("first", -1)
            with engine.Fori(0, B - 1) as b:
                emit("body", b)
            emit("last", B - 1)

        def wait_apart(engine, semaphore, count):
            if not isinstance(count, int):
                engine.compute_val(count)
            engine.wait_ge(started, 1)
            engine.wait_ge(semaphore, count)

        def chunk(ch):
            return slice(CH * ch, CH * (ch + 1))

        @block.sync
        def _(sp):
            sp.dma_start(xa[:], x_tiles[0]).then_inc(xa_loaded, 16)
            sp.dma_start(w_dq_sb, w_dq.rearrange("(t p) c -> p t c", p=P)).then_inc(proj_loaded, 16)
            sp.dma_start(w_uq_sb, w_uq_t.rearrange("(t p) c -> p t c", p=P)).then_inc(proj_loaded, 16)
            sp.dma_start(ident[:], identity).then_inc(proj_loaded, 16)
            sp.wait_ge(pads_ready, 1)
            sp.dma_start(wdkv[:, :, 0:CKV], w_dkv_t.rearrange("(t p) c -> p t c", p=P)).then_inc(proj_loaded, 16)
            sp.dma_start(wuk[0:CKV, :], w_uk_t).then_inc(proj_loaded, 16)
            sp.dma_start(wuv[0:CKV, :], w_uv_t).then_inc(proj_loaded, 16)
            for dst, src in (
                (w_raw[:, :, 0:J], w_up_t.rearrange("(t p) j -> p t j", p=P)),
                (w_raw[:, :, J:2 * J], w_gate_t.rearrange("(t p) j -> p t j", p=P)),
                (d_mix[0].rearrange("p (t c) -> p t c", c=D), w_down_t.rearrange("(t p) c -> p t c", p=P)),
                (hada[:], hadamard), (mask[:], causal),
                (signs_ug[:], su_ug),
                (signs_dp[:], su_dp),
                (scale_ug, wscale_ug.partition_broadcast(P)), (scale_dp, wscale_dp.partition_broadcast(P)),
                (bo[:], b_o.partition_broadcast(P)), (wo[:], w_o_t.rearrange("(t p) c -> p t c", p=P)),
            ):
                sp.dma_start(dst, src).then_inc(ffn_loaded, 16)

            sp.dma_start(k_stack[KS:KM], ones).then_inc(ones_loaded, 16)

            def store_parts(i, which):
                scratch = (q_scratch, k_scratch)[which]
                wait_apart(sp, part2_ready, 8 * i + 4 * which + 4)
                if not (isinstance(i, int) and i == 0):
                    wait_apart(sp, early_loaded, 16 * STACK_LOADS * i)
                    wait_apart(sp, late_loaded, 16 * STACK_LOADS * i)
                for s in range(3):
                    sp.dma_start(scratch[s].rearrange("(t h) p n -> (h p) t n", t=DT), parts[:, s])\
                      .then_inc(parts_stored, 16)

            def load_stack(i, which, heads, loaded):
                stack, scratch = ((q_stack, q_scratch), (k_stack, k_scratch))[which]
                sp.wait_ge(parts_stored, 48 * (2 * i + which + 1))
                for s, pair in enumerate(STRIPS):
                    sp.dma_start(stack[DH * s:DH * (s + 1), heads],
                                 scratch[pair[which]][heads].rearrange("h p n -> p h n")).then_inc(loaded, 16)

            def after_scores(segment, b, *step):
                if segment == "body":
                    slot, before = turns.of(segment, b, "st", *step)
                    wait_apart(sp, psum_filled[slot], before + 1)

            def emit(segment, b):
                for step in results(segment):
                    kind = step[0]
                    if kind in ("q", "k") and step[1:] == (DT - 1, NCH - 1):
                        which = 0 if kind == "q" else 1
                        store_parts(b + 1, which)
                        after_scores(segment, b, QUADS - 1, KEY_TILES[0], 0)
                        load_stack(b + 1, which, slice(0, H - QUAD), early_loaded)
                    if kind == "stack":
                        after_scores(segment, b, QUADS - 1, KEY_TILES[-1], QUAD - 1)
                        for which in range(2):
                            load_stack(b + 1, which, slice(H - QUAD, H), late_loaded)
                    if kind == "mt":
                        _, ahead, quad = step
                        sp.wait_ge(max_parts_ready, QUADS * (b + ahead) + quad + 1)
                        for j in range(3):
                            row = q_stack[KS + j:KS + j + 1, QUAD * quad:QUAD * (quad + 1), :]
                            sp.dma_start(row.rearrange("o h (t n) -> o (h t) n", n=P), max_parts[:, j, :])\
                              .then_inc(max_loaded, 16)
                    if step == ("st", 0, 0, 0) and segment == "body":
                        slot, before = turns.of(segment, b, *step)
                        wait_apart(sp, psum_filled[slot], before + 1)
                        sp.dma_start(xa[:], x_tiles[b + 1]).then_inc(xa_loaded, 16)
                    if kind == "fin":
                        t = TC * step[1] + step[2]
                        wait_apart(sp, out_ready, b * TT + t + 1)
                        sp.dma_start(out_tiles[b, t], xr[:, t, :]).then_inc(out_stored, 16)
                if segment == "first":
                    sp.wait_ge(folded, FOLDS[0])
                    sp.dma_start(xr[:], x_tiles[0]).then_inc(xr_loaded, 16)
                if segment == "body":
                    wait_apart(sp, out_stored, 16 * TT * (b + 1))
                    sp.dma_start(xr[:], x_tiles[b + 1]).then_inc(xr_loaded, 16)

            segments(sp, emit)
            sp.wait_ge(out_stored, 16 * TT * B)

        @block.gpsimd
        def _(pool):
            nc.gpsimd.memset(minus_half[:], -0.5).then_inc(started, 1)
            nc.gpsimd.memset(zeros[:], 0.0)
            nc.gpsimd.memset(wdkv[:], 0.0)
            nc.gpsimd.memset(wuk[:], 0.0)
            nc.gpsimd.memset(wuv[:], 0.0).then_inc(pads_ready, 1)
            nc.gpsimd.memset(v_ones[:, :, H * VW:], 0.0)
            nc.gpsimd.memset(v_ones[:, :, 0:H * VW].rearrange("p t (h w) -> p t h w", w=VW)[:, :, :, DH:VW], 1.0)\
              .then_inc(pads_ready, 1)

            def root(key, rows, n):
                before = ROOT_STEPS[key] * (n - 1)
                nc.gpsimd.tensor_scalar(var_eps[key][:, rows], mv[key][:, rows, 1], EPS, None, ALU.add)\
                  .then_inc(root_steps[key], 1)
                pool.wait_ge(root_steps[key], before + 1)
                nc.gpsimd.tensor_tensor(rstd[key][:, rows], var_eps[key][:, rows], minus_half[:, rows], ALU.pow)\
                  .then_inc(root_steps[key], 1)
                if key == "ln1":
                    return
                pool.wait_ge(root_steps[key], before + 2)
                nc.gpsimd.tensor_tensor(scaled_mean[:, rows], mv[key][:, rows, 0], rstd[key][:, rows], ALU.mult)\
                  .then_inc(root_steps[key], 1)
                pool.wait_ge(root_steps[key], before + 3)
                nc.gpsimd.tensor_tensor(shift[key][:, rows], (shift["lna"] if key == "lnf" else zeros)[:, rows],
                                        scaled_mean[:, rows], ALU.subtract).then_inc(root_steps[key], 1)

            pool.wait_ge(pads_ready, 2)

            def emit(segment, b):
                splits = 0
                for step in results(segment):
                    kind = step[0]
                    if kind == "ln1":
                        wait_apart(pool, ln1_stats, b + 2)
                        root("ln1", slice(0, TT), b + 2)
                    if kind in ("wug", "wd"):
                        slot, before = turns.of(segment, b, *step)
                        pool.wait_ge(psum_taken[slot], before + 1)
                    if kind == "wug":
                        w = wug[:, step[1], chunk(step[2])]
                        nc.gpsimd.tensor_tensor(w, w, scale_ug[:, chunk(step[2])], ALU.mult).then_inc(folded, 1)
                    if kind == "wd":
                        for jt in (2 * step[1], 2 * step[1] + 1):
                            last = nc.gpsimd.tensor_tensor(wd[:, jt, :], wd[:, jt, :], scale_dp, ALU.mult)
                        last.then_inc(folded, 1)
                    if kind in ("q", "k"):
                        _, dt, ch = step
                        pool.wait_ge(part1_ready, 8 * (b + 1) + splits + 1)
                        nc.gpsimd.tensor_tensor(parts[:, 2, dt, chunk(ch)], rest[:, splits % 2],
                                                parts[:, 1, dt, chunk(ch)], ALU.subtract).then_inc(part2_ready, 1)
                        splits += 1
                    if kind == "st":
                        _, quad, kt, h = step
                        slot, before = turns.of(segment, b, *step)
                        if h < QUAD - 2:
                            continue
                        wait_apart(pool, psum_taken[slot], before + 1)
                        if h < QUAD - 1:
                            continue
                        column = probs_column(kt, kt * P)
                        tile = probs[:, probs_half(kt), :, column:column + P]
                        nc.gpsimd.affine_select(out=tile, in_=tile, compare_op=ALU.is_ge, fill=0.0, base=0,
                                                pattern=[[0, QUAD], [1, P]], channel_multiplier=-1).then_inc(masked, 1)
                    if kind == "ln2" and step[2] < 2:
                        _, ch, phase = step
                        wait_apart(pool, ln2_stats, b * 2 * NCH + 2 * ch + phase + 1)
                        root(("lna", "lnx")[phase], slice(TC * ch, TC * (ch + 1)), b * NCH + ch + 1)
                    if kind == "dn":
                        t = TC * step[1] + step[2]
                        wait_apart(pool, ln3_stats, b * TT + t + 1)
                        root("lnf", slice(t, t + 1), b * TT + t + 1)
                    if kind == "fin":
                        t = TC * step[1] + step[2]
                        pool.wait_ge(ffn_ready, b * TT + t + 1)
                        nc.gpsimd.tensor_tensor(xr[:, t, :], xr[:, t, :], ffn_n[:, t % 2], ALU.add)\
                          .then_inc(out_ready, 1)

            segments(pool, emit)

        @block.scalar
        def _(act):
            def emit(segment, b):
                splits = 0
                for step in results(segment):
                    kind = step[0]
                    if kind in ("wq", "xt", "x2t", "q", "k", "ckv", "v", "st", "cn", "dn",
                                "wug", "wd"):
                        slot, before = turns.of(segment, b, *step)
                        src = psum[slot]
                    if kind in ("q", "k") and splits % 4 == 0:
                        wait_past(act, parts_stored, 48 * (2 * (b + 1) + splits // 4))
                    if step == ("gate", 0, 0):
                        act.wait_ge(parts_stored, 48 * 2 * (b + 2 if segment == "body" else B))
                    if step == ("cn", 0):
                        act.wait_ge(folded, sum(FOLDS))
                    if kind in ("wq", "xt", "x2t", "q", "k", "ckv", "v", "st", "cn", "dn", "wug", "wd"):
                        act.wait_ge(psum_filled[slot], before + 1)
                    if kind == "wug":
                        _, c, n = step
                        nc.scalar.activation(wug[:, c, chunk(n)], src[:, 0:CH], ACT.Identity, scale=signs_ug[:, c:c + 1])\
                          .then_inc(psum_taken[slot], 1)
                    if kind == "wd":
                        for i in range(2):
                            jt = 2 * step[1] + i
                            last = nc.scalar.activation(wd[:, jt, :], src[:, D * i:D * (i + 1)], ACT.Identity,
                                                        scale=signs_dp[:, jt:jt + 1])
                        last.then_inc(psum_taken[slot], 1)
                    if kind == "wq":
                        nc.scalar.activation(wq[:].rearrange("p c d -> p (c d)"), src[:], ACT.Copy)\
                          .then_inc(psum_taken[slot], 1)
                    if kind in ("xt", "x2t"):
                        _, ch, c = step
                        nc.scalar.activation(xT[:, c, chunk(ch)], src[:], ACT.Copy).then_inc(psum_taken[slot], 1)
                    if kind in ("q", "k"):
                        _, dt, ch = step
                        nc.scalar.activation(parts[:, 0, dt, chunk(ch)], src[:], ACT.Copy).then_inc(part0_ready, 1)
                        splits += 1
                    if kind == "ckv":
                        nc.scalar.activation(ckvT[:, chunk(step[1])], src[:], ACT.Copy).then_inc(psum_taken[slot], 1)
                    if kind == "v":
                        n = step[1]
                        dst = v_ones[:, 2 * n:2 * n + 2, 0:H * VW].rearrange("p t (h w) -> p t h w", w=VW)
                        nc.scalar.activation(dst[:, :, :, 0:DH], src[:].rearrange("p (t h w) -> p t h w", t=2, w=DH),
                                             ACT.Copy).then_inc(psum_taken[slot], 1)
                    if kind == "st":
                        _, quad, kt, h = step
                        column = probs_column(kt, kt * P)
                        nc.scalar.activation(probs[:, probs_half(kt), h, column:column + N - kt * P],
                                             src[:, kt * P:], ACT.Exp,
                                             scale=DH ** -0.5).then_inc(psum_taken[slot], 1)
                    if kind == "pv" and step[2] == LAST_KEYS[step[3]]:
                        _, quad, _, half = step
                        slot, before = turns.of(segment, b, "pv", quad, half)
                        act.wait_ge(psum_filled[slot], before + 1)
                        nc.scalar.activation(ctx_raw[:, quad, chunk(half)], psum[slot][:], ACT.Copy)\
                          .then_inc(psum_taken[slot], 1)
                    if kind == "cn":
                        nc.scalar.activation(ctx_nT[:, step[1] % 2], src[:, 0:D], ACT.Copy)\
                          .then_inc(psum_taken[slot], 1)
                    if kind == "gate":
                        _, ch, jt = step
                        src = psum[turns.of(segment, b, "gu", ch, jt)[0]]
                        act.wait_ge(gate_filled, b * NCH * JT + JT * ch + jt + 1)
                        nc.scalar.activation(tanh_g[:, jt % 2], src[:, 0:CH], ACT.Tanh, scale=0.5)\
                          .then_inc(tanh_ready, 1)
                    if kind == "ln2" and step[2] == 2:
                        ch = step[1]
                        act.wait_ge(root_steps["lnx"], ROOT_STEPS["lnx"] * (b * NCH + ch + 1))
                        for t in range(TC * ch, TC * (ch + 1)):
                            last = nc.scalar.activation(y[:, t, :], xr[:, t, :], ACT.Identity,
                                                        bias=shift["lnx"][:, t:t + 1], scale=rstd["lnx"][:, t:t + 1])
                        last.then_inc(x2n_ready, 1)
                    if kind == "dn":
                        t = TC * step[1] + step[2]
                        if t > 1:
                            act.wait_ge(ffn_ready, b * TT + t - 1)
                        nc.scalar.activation(ffn_raw[:, t % 2], src[:, 0:D], ACT.Copy).then_inc(psum_taken[slot], 1)
                    if kind == "fin":
                        t = TC * step[1] + step[2]
                        act.wait_ge(root_steps["lnf"], ROOT_STEPS["lnf"] * (b * TT + t + 1))
                        if t > 1:
                            act.wait_ge(out_ready, b * TT + t - 1)
                        nc.scalar.activation(ffn_n[:, t % 2], ffn_raw[:, t % 2], ACT.Identity,
                                             bias=shift["lnf"][:, t:t + 1], scale=rstd["lnf"][:, t:t + 1])\
                          .then_inc(ffn_ready, 1)

            segments(act, emit)

        @block.vector
        def _(dve):
            def moments(key, tile, source):
                return nc.vector.bn_stats(stats[key][:, tile, :], source)

            def aggregate(key, tile):
                return nc.vector.bn_aggr(mv[key][:, tile, :], stats[key][:, tile, :])

            def normalise(dst, source, key, t):
                return nc.vector.tensor_scalar(dst, source, mv[key][:, t, 0:1], rstd[key][:, t:t + 1],
                                               ALU.subtract, ALU.mult)

            def emit(segment, b):
                links.start(segment, b)
                splits = 0
                for step in results(segment):
                    kind = step[0]
                    if kind in ("sa", "mt", "q", "k", "ct", "wo", "gu", "dn"):
                        slot, before = turns.of(segment, b, *step)
                        src = psum[slot]
                        if kind == "sa":
                            wait_apart(dve, psum_filled[slot], before + 1)
                        elif kind not in ("mt", "q", "k", "dn"):
                            dve.wait_ge(psum_filled[slot], before + 1)
                    if kind == "sa":
                        _, _, quad, h, qt, k0, keys, _ = step
                        if k0 + keys < (qt + 1) * P:
                            nc.vector.tensor_reduce(row_max0[:, h, qt - TC:qt - TC + 1], src[:, 0:keys], AX_X, ALU.max)\
                              .then_inc(psum_taken[slot], 1)
                        else:
                            nc.vector.tensor_tensor_reduce(src[:, 0:keys], src[:, 0:keys], mask[:, CH - keys:CH],
                                                           1.0, MASKED, ALU.add, ALU.max,
                                                           row_max[:, h, qt:qt + 1]).then_inc(psum_taken[slot], 1)
                            last_piece = slot, before
                    if kind == "mt":
                        _, ahead, quad = step
                        dve.wait_ge(psum_taken[last_piece[0]], last_piece[1] + 1)
                        nc.vector.tensor_tensor(row_max[:, :, TC:TT], row_max[:, :, TC:TT], row_max0[:], ALU.max)\
                          .then_inc(row_max_ready, 1)
                        dve.wait_ge(psum_filled[slot], before + 1)
                        wait_past(dve, max_loaded, 48 * (QUADS * (b + ahead) + quad))
                        done = links.count()
                        nc.vector.tensor_scalar(max_parts[:, 0, :], src[0:QUAD * TT, 0:P], -1.0, None, ALU.mult)\
                          .then_inc(dve_done, 1)
                        dve.wait_ge(dve_done, done)
                        done = links.count()
                        nc.vector.scalar_tensor_tensor(out=max_rest[:], in0=src[0:QUAD * TT, 0:P], scalar=-1.0,
                                                       in1=max_parts[:, 0, :], op0=ALU.mult, op1=ALU.subtract)\
                          .then_inc(psum_taken[slot], 1)
                        dve.wait_ge(psum_taken[slot], before + 1)
                        nc.vector.tensor_copy(max_parts[:, 1, :], max_rest[:]).then_inc(dve_done, 1)
                        dve.wait_ge(dve_done, done)
                        nc.vector.tensor_tensor(max_parts[:, 2, :], max_rest[:], max_parts[:, 1, :], ALU.subtract)\
                          .then_inc(max_parts_ready, 1)
                    if kind == "ln1":
                        dve.wait_ge(xa_loaded, 16 * (b + 2))
                        for t in range(TT):
                            last = moments("ln1", t, xa[:, t, :])
                        done = links.count()
                        last.then_inc(dve_done, 1)
                        wait_apart(dve, dve_done, done)
                        for t in range(TT):
                            last = aggregate("ln1", t)
                        last.then_inc(ln1_stats, 1)
                        dve.wait_ge(ln1_stats, b + 2)
                        dve.wait_ge(root_steps["ln1"], ROOT_STEPS["ln1"] * (b + 2))
                        for t in range(TT):
                            last = normalise(xa[:, t, :], xa[:, t, :], "ln1", t)
                        last.then_inc(xn_ready, 1)
                    if kind in ("q", "k"):
                        _, dt, ch = step
                        n = 8 * (b + 1) + splits
                        if splits > 1:
                            dve.wait_ge(part2_ready, n - 1)
                        dve.wait_ge(part0_ready, n + 1)
                        nc.vector.tensor_tensor(rest[:, splits % 2], src[:], parts[:, 0, dt, chunk(ch)], ALU.subtract)\
                          .then_inc(psum_taken[slot], 1)
                        dve.wait_ge(psum_taken[slot], before + 1)
                        nc.vector.tensor_copy(parts[:, 1, dt, chunk(ch)], rest[:, splits % 2])\
                          .then_inc(part1_ready, 1)
                        splits += 1
                    if kind == "ct":
                        t = step[1]
                        heads = src[:, 0:CH].rearrange("p (h w) -> p h w", h=H)
                        done = links.count()
                        nc.vector.reciprocal(rden[:, t % 2, :], heads[:, :, DH]).then_inc(dve_done, 1)
                        dve.wait_ge(dve_done, done)
                        if t > 1:
                            other, uses = turns.of(segment, b, "cn", t - 2)
                            dve.wait_ge(psum_filled[other], uses + 1)
                        nc.vector.tensor_tensor(ctx_n[:, t % 2].rearrange("p (h w) -> p h w", h=H), heads[:, :, 0:DH],
                                                rden[:, t % 2, :].unsqueeze(2).broadcast_to((P, H, DH)), ALU.mult)\
                          .then_inc(psum_taken[slot], 1)
                    if kind == "wo":
                        t = step[1]
                        nc.vector.tensor_tensor(y[:, t, :], src[:, 0:D], bo[:], ALU.add).then_inc(psum_taken[slot], 1)
                        dve.wait_ge(psum_taken[slot], before + 1)
                        done = links.count()
                        moments("lna", t, y[:, t, :]).then_inc(dve_done, 1)
                    if kind == "ln2" and step[2] == 0:
                        ch = step[1]
                        wait_apart(dve, dve_done, done)
                        for t in range(TC * ch, TC * (ch + 1)):
                            last = aggregate("lna", t)
                        last.then_inc(ln2_stats, 1)
                    if kind == "ln2" and step[2] == 1:
                        ch = step[1]
                        tiles = range(TC * ch, TC * (ch + 1))
                        dve.wait_ge(root_steps["lna"], ROOT_STEPS["lna"] * (b * NCH + ch) + 2)
                        dve.wait_ge(xr_loaded, 16 * (b + 1))
                        for t in tiles:
                            last = nc.vector.scalar_tensor_tensor(out=xr[:, t, :], in0=y[:, t, :],
                                                                  scalar=rstd["lna"][:, t:t + 1], in1=xr[:, t, :],
                                                                  op0=ALU.mult, op1=ALU.add)
                        done = links.count()
                        last.then_inc(dve_done, 1)
                        dve.wait_ge(dve_done, done)
                        for t in tiles:
                            last = moments("lnx", t, xr[:, t, :])
                        done = links.count()
                        last.then_inc(dve_done, 1)
                        wait_apart(dve, dve_done, done)
                        for t in tiles:
                            last = aggregate("lnx", t)
                        last.then_inc(ln2_stats, 1)
                    if kind == "gu":
                        _, ch, jt = step
                        dve.wait_ge(tanh_ready, b * NCH * JT + JT * ch + jt + 1)
                        done = links.count()
                        nc.vector.scalar_tensor_tensor(out=gated[:, jt % 2], in0=tanh_g[:, jt % 2], scalar=1.0,
                                                       in1=src[:, 0:CH], op0=ALU.add, op1=ALU.mult)\
                          .then_inc(dve_done, 1)
                        dve.wait_ge(dve_done, done)
                        nc.vector.tensor_tensor(hT[ch][:, jt, :], gated[:, jt % 2], src[:, CH:2 * CH], ALU.mult)\
                          .then_inc(psum_taken[slot], 1)
                    if kind == "dn":
                        t = TC * step[1] + step[2]
                        wait_apart(dve, psum_taken[slot], before + 1)
                        done = links.count()
                        moments("lnf", t, ffn_raw[:, t % 2]).then_inc(dve_done, 1)
                        wait_apart(dve, dve_done, done)
                        aggregate("lnf", t).then_inc(ln3_stats, 1)
                    if step == ("mix", 0):
                        dve.wait_ge(ffn_loaded, 16 * 11)
                        nc.vector.tensor_tensor(w_mix[:, 0], w_raw[:, 0], w_raw[:, 1], ALU.add)
                        nc.vector.tensor_tensor(w_mix[:, 1], w_raw[:, 0], w_raw[:, 1], ALU.subtract)
                        nc.vector.tensor_scalar(signs_ug[:], signs_ug[:], D ** -0.5, None, ALU.mult)
                        nc.vector.tensor_scalar(signs_dp[:], signs_dp[:], 0.5 * J ** -0.5, None, ALU.mult)\
                          .then_inc(w_mixed, 1)
                    if step == ("mix", 1):
                        for stage in range(3):
                            a, z = (m.rearrange("p (o two s) -> p o two s", two=2, s=D << stage)
                                    for m in (d_mix[stage % 2], d_mix[1 - stage % 2]))
                            dve.wait_ge(w_mixed, 1 + stage)
                            nc.vector.tensor_tensor(z[:, :, 0], a[:, :, 0], a[:, :, 1], ALU.add)
                            nc.vector.tensor_tensor(z[:, :, 1], a[:, :, 0], a[:, :, 1], ALU.subtract)\
                              .then_inc(w_mixed, 1)

            segments(dve, emit)

        @block.tensor
        def _(pe):
            def emit(segment, b):
                for step in schedule(segment):
                    kind = step[0]
                    if kind in RING:
                        part = step[3] if kind in ("gu", "dn") else 0
                        step = step[:3] if kind in ("gu", "dn") else step
                        slot, before = turns.of(segment, b, *step)
                        dst = psum[slot]
                        if kind != "mt" and part == 0:
                            wait_past(pe, psum_taken[slot], before)
                    if kind == "wq":
                        pe.wait_ge(proj_loaded, 16 * 6)
                        for ct in range(DT):
                            for t in range(DT):
                                last = nc.tensor.matmul(dst[:, D * ct:D * (ct + 1)], w_dq_sb[:, t, P * ct:P * (ct + 1)],
                                                        w_uq_sb[:, t, :], start=(t == 0), stop=(t == DT - 1))
                        last.then_inc(psum_filled[slot], 1)
                    if kind == "xt":
                        _, ch, c = step
                        pe.wait_ge(xn_ready, b + 2)
                        for t in range(TC):
                            last = nc.tensor.transpose(dst[:, P * t:P * (t + 1)],
                                                       xa[:, TC * ch + t, P * c:P * (c + 1)], ident[:])
                        last.then_inc(psum_filled[slot], 1)
                    if kind in ("q", "ckv"):
                        dt, ch = (step[1], step[2]) if kind == "q" else (0, step[1])
                        wait_taken(segment, b, slot, *(("xt", ch, c) for c in range(DT)))
                        if (kind, dt, ch) == ("q", 0, 0) and segment == "first":
                            wait_taken(segment, b, slot, ("wq",))
                        for c in range(DT):
                            w = wq[:, c, P * dt:P * (dt + 1)] if kind == "q" else wdkv[:, c, :]
                            last = nc.tensor.matmul(dst[:], w, xT[:, c, chunk(ch)], start=(c == 0), stop=(c == DT - 1))
                        last.then_inc(psum_filled[slot], 1)
                    if kind == "v":
                        n = step[1]
                        wait_taken(segment, b, slot, ("ckv", 2 * n // TC))
                        for i in range(2):
                            t = 2 * n + i
                            last = nc.tensor.matmul(dst[:, D * i:D * (i + 1)], ckvT[:, P * t:P * (t + 1)], wuv[:],
                                                    start=True, stop=True)
                        last.then_inc(psum_filled[slot], 1)
                    if kind == "k":
                        _, dt, ch = step
                        wait_taken(segment, b, slot, ("ckv", ch))
                        nc.tensor.matmul(dst[:], wuk[:, P * dt:P * (dt + 1)], ckvT[:, chunk(ch)], start=True, stop=True)\
                          .then_inc(psum_filled[slot], 1)
                    if kind == "sa":
                        _, ahead, quad, h, qt, k0, keys, _ = step
                        head = QUAD * quad + h
                        if (h, qt, k0) == (0, 0, 0) and quad in (0, QUADS - 1):
                            loaded = early_loaded if quad == 0 else late_loaded
                            pe.wait_ge(loaded, 16 * STACK_LOADS * (b + ahead + 1))
                        nc.tensor.matmul(dst[:, 0:keys], q_stack[0:KS, head, P * qt:P * (qt + 1)],
                                         k_stack[0:KS, head, k0:k0 + keys], start=True, stop=True)\
                          .then_inc(psum_filled[slot], 1)
                    if kind == "mt":
                        _, ahead, quad = step
                        pe.wait_ge(row_max_ready, QUADS * (b + ahead) + quad + 1)
                        wait_past(pe, psum_taken[slot], before)
                        nc.tensor.transpose(dst[0:QUAD * TT, 0:P], row_max[:].rearrange("p h t -> p (h t)"), ident[:])\
                          .then_inc(psum_filled[slot], 1)
                    if kind == "st":
                        _, quad, kt, h = step
                        head = QUAD * quad + h
                        if (kt, h) == (0, 0):
                            pe.wait_ge(max_loaded, 48 * (QUADS * b + quad + 1))
                        for q0 in range(kt * P // CH * CH, N, CH):
                            cols = slice(max(q0, kt * P), q0 + CH)
                            last = nc.tensor.matmul(dst[:, cols], k_stack[0:KM, head, P * kt:P * (kt + 1)],
                                                    q_stack[0:KM, head, cols], start=True, stop=True)
                        last.then_inc(psum_filled[slot], 1)
                    if kind == "pv":
                        _, quad, kt, half = step
                        slot, before = turns.of(segment, b, "pv", quad, half)
                        if kt == 0:
                            wait_past(pe, psum_taken[slot], before)
                        pe.wait_ge(masked, (b * QUADS + quad) * TT + place_of(kt) + 1)
                        q0 = max(CH * half, kt * P)
                        columns = slice(probs_column(kt, q0), probs_column(kt, CH * (half + 1)))
                        last_keys = kt == LAST_KEYS[half]
                        for h in range(QUAD):
                            col = VW * (QUAD * quad + h)
                            last = nc.tensor.matmul(psum[slot][32 * h:32 * (h + 1), q0 - CH * half:CH],
                                                    v_ones[:, kt, col:col + 32], probs[:, probs_half(kt), h, columns],
                                                    start=(kt == 0), stop=last_keys, skip_group_check=True)
                        if last_keys:
                            last.then_inc(psum_filled[slot], 1)
                    if kind == "ct":
                        t = step[1]
                        if t % TC == 0:
                            wait_taken(segment, b, slot, ("pv", QUADS - 1, t // TC))
                        for quad in range(QUADS):
                            last = nc.tensor.transpose(dst[:, P * quad:P * (quad + 1)],
                                                       ctx_raw[:, quad, P * t:P * (t + 1)], ident[:])
                        last.then_inc(psum_filled[slot], 1)
                    if kind == "cn":
                        t = step[1]
                        wait_taken(segment, b, slot, ("ct", t))
                        for c in range(DT):
                            last = nc.tensor.transpose(dst[:, P * c:P * (c + 1)], ctx_n[:, t % 2, P * c:P * (c + 1)],
                                                       ident[:])
                        last.then_inc(psum_filled[slot], 1)
                    if kind == "wo":
                        t = step[1]
                        wait_taken(segment, b, slot, ("cn", t))
                        for c in range(DT):
                            last = nc.tensor.matmul(dst[:, 0:D], ctx_nT[:, t % 2, P * c:P * (c + 1)], wo[:, c, :],
                                                    start=(c == 0), stop=(c == DT - 1))
                        last.then_inc(psum_filled[slot], 1)
                    if kind == "x2t":
                        _, ch, c = step
                        pe.wait_ge(x2n_ready, b * NCH + ch + 1)
                        for t in range(TC):
                            last = nc.tensor.transpose(dst[:, P * t:P * (t + 1)], y[:, TC * ch + t, P * c:P * (c + 1)],
                                                       ident[:])
                        last.then_inc(psum_filled[slot], 1)
                    if kind == "gu":
                        _, ch, jt = step
                        if (ch, jt, part) == (0, 0, 0):
                            pe.wait_ge(folded, sum(FOLDS))
                        if part == 0:
                            wait_taken(segment, b, slot, *(("x2t", ch, c) for c in range(DT)))
                        i, c = divmod(part, DT)
                        j0 = (J, 0)[i] + P * jt
                        last = nc.tensor.matmul(dst[:, CH * i:CH * (i + 1)], wug[:, c, j0:j0 + P], xT[:, c, chunk(ch)],
                                                start=(c == 0), stop=(c == DT - 1))
                        if part == GATE_PART:
                            last.then_inc(gate_filled, 1)
                        if part == PARTS - 1:
                            last.then_inc(psum_filled[slot], 1)
                    if kind == "dn":
                        _, ch, t = step
                        if part == 0:
                            wait_taken(segment, b, slot, ("gu", ch, JT - 1))
                        for jt in range(JT // PARTS * part, JT // PARTS * (part + 1)):
                            last = nc.tensor.matmul(dst[:, 0:D], hT[ch][:, jt, P * t:P * (t + 1)], wd[:, jt, :],
                                                    start=(jt == 0), stop=(jt == JT - 1))
                        if part == PARTS - 1:
                            last.then_inc(psum_filled[slot], 1)
                    if kind in ("wug", "wd"):
                        if step == ("wug", 0, 0):
                            pe.wait_ge(ffn_loaded, 16 * 11)
                        pe.wait_ge(w_mixed, 1 if kind == "wug" else 4)
                        rhs = w_mix[:, step[1], chunk(step[2])] if kind == "wug" else d_mix[1][:, chunk(step[1])]
                        nc.tensor.matmul(dst[:, 0:CH], hada[:], rhs, start=True, stop=True).then_inc(psum_filled[slot], 1)
                if segment == "first":
                    pe.wait_ge(ones_loaded, 16)
                    pe.wait_ge(pads_ready, 2)

            def wait_taken(segment, b, own, *steps):
                places = dict(turns.of(segment, b, *step) for step in steps)
                for slot, before in places.items():
                    if slot != own:
                        pe.wait_ge(psum_taken[slot], before + 1)

            segments(pe, emit)



def kernel(**inputs):
    import numpy as np
    import concourse.bacc as bacc
    from concourse.bass_utils import run_bass_kernel_spmd

    a = {k[3:]: np.asarray(v) for k, v in inputs.items()}
    sylvester = np.ones((1, 1), np.float32)
    while len(sylvester) < P:
        sylvester = np.block([[sylvester, sylvester], [sylvester, -sylvester]])
    bf16 = mybir.dt.np(BF16)
    causal = np.zeros((P, CH), np.float32)
    causal[:, CH - P:] = np.where(np.arange(P)[None, :] > np.arange(P)[:, None], MASKED, 0.0)
    arrays = {
        "x": a["attn_x"], "w_dq": a["attn_W_DQ"], "w_uq_t": a["attn_W_UQ"].T, "w_dkv_t": a["attn_W_DKV"].T,
        "w_uk_t": a["attn_W_UK"].T, "w_uv_t": a["attn_W_UV"].T, "w_o_t": a["attn_W_O"].T, "b_o": a["attn_b_O"],
        "su_ug": a["ffn_SU_ug"].reshape(DT, P).T, "su_dp": a["ffn_SU_dp"].reshape(JT, P).T, "wscale_ug": a["ffn_Wscale_ug"],
        "wscale_dp": a["ffn_Wscale_dp"], "w_up_t": a["ffn_W_up"].T, "w_gate_t": a["ffn_W_gate"].T,
        "w_down_t": a["ffn_W_down"].T, "hadamard": sylvester, "identity": np.eye(P, dtype=np.float32),
        "causal": causal.astype(bf16), "ones": np.ones((KM - KS, H, N), bf16),
    }
    arrays = {k: np.ascontiguousarray(v) for k, v in arrays.items()}
    nc = bacc.Bacc("TRN2", target_bir_lowering=False, num_devices=1)
    args = [nc.dram_tensor(k, v.shape, mybir.dt.from_np(v.dtype), kind="ExternalInput").ap()
            for k, v in arrays.items()]
    args.append(nc.dram_tensor("out", (B, N, D), F32, kind="ExternalOutput").ap())
    layer(nc, *args)
    result = run_bass_kernel_spmd(nc, [arrays], core_ids=[0])
    return result.results[0]["out"]
```
